# Optimizing a Trainium2 kernel written in Bass

```python
import numpy as np
import jax
import jax.numpy as jnp

def _softmax(x, axis=-1):
    return jax.nn.softmax(x, axis=axis)
def _gelu(x):
    return jax.nn.gelu(x, approximate=True)
def _silu(x):
    return jax.nn.silu(x)
def _sigmoid(x):
    return jax.nn.sigmoid(x)
def _layernorm(x, axis=-1, eps=1e-5):
    m = jnp.mean(x, axis=axis, keepdims=True)
    v = jnp.var(x, axis=axis, keepdims=True)
    return (x - m) / jnp.sqrt(v + eps)
def _scatter_add(tgt, idx, src, axis=0):
    return tgt.at[idx].add(src)
def _segment_sum(src, seg, n):
    return jax.ops.segment_sum(src, seg, n)

kernel_name = 'mk_conv_seq_d4_conv_nchw128_962532'

def setup_inputs(seed: int = 0):
    np.random.seed(seed)
    _w = jnp.asarray
    def _rec_inputs():
        import jax
        import jax.numpy as jnp
        _gk = jax.random.key(seed)
        x = -0.0005207 + 1.001 * jax.random.normal(jax.random.fold_in(_gk, 1), (4, 128, 64, 64), jnp.float32)
        return x
    x = _rec_inputs()
    def _L0_conv_setup():
        import jax, jax.numpy as jnp
        import numpy as np
        from jax import lax
        B_, C_, H_, W_ = (4, 128, 64, 64)
        D_INNER, D_STATE, DT_RANK, D_CONV = (256, 16, 8, 4)

        def _mamba2d(x, proj_w, in_proj_w, conv_w, conv_b, x_proj_w, dt_proj_w, dt_proj_b, A_log, D, out_proj_w):
            b, c, h, w = x.shape
            L = h * w
            u = jnp.einsum('oc,bchw->bohw', proj_w, x).reshape(b, c, L).transpose(0, 2, 1)
            xz = u @ in_proj_w.T
            xs, zg = (xz[..., :D_INNER], xz[..., D_INNER:])
            xt = xs.transpose(0, 2, 1)
            xt = lax.conv_general_dilated(xt, conv_w, window_strides=(1,), padding=[(D_CONV - 1, 0)], feature_group_count=D_INNER)
            xc = jax.nn.silu(xt + conv_b[None, :, None]).transpose(0, 2, 1)
            x_dbl = xc @ x_proj_w.T
            dt_r = x_dbl[..., :DT_RANK]
            Bm = x_dbl[..., DT_RANK:DT_RANK + D_STATE]
            Cm = x_dbl[..., DT_RANK + D_STATE:]
            delta = jax.nn.softplus(dt_r @ dt_proj_w.T + dt_proj_b)
            A = -jnp.exp(A_log)

            def step(hprev, inp):
                dt_t, B_t, C_t, x_t = inp
                dA = jnp.exp(dt_t[:, :, None] * A)
                hn = dA * hprev + (dt_t * x_t)[:, :, None] * B_t[:, None, :]
                y = jnp.einsum('bdn,bn->bd', hn, C_t)
                return (hn, y)
            h0 = jnp.zeros((b, D_INNER, D_STATE), xc.dtype)
            _, ys = lax.scan(step, h0, (delta.transpose(1, 0, 2), Bm.transpose(1, 0, 2), Cm.transpose(1, 0, 2), xc.transpose(1, 0, 2)))
            y = ys.transpose(1, 0, 2) + xc * D
            y = y * jax.nn.silu(zg)
            out = y @ out_proj_w.T
            return out.transpose(0, 2, 1).reshape(b, c, h, w) + x
        ks = jax.random.split(jax.random.key(seed), 12)

        def rn(k, shape, fan_in):
            return jax.random.normal(k, shape, jnp.float32) * fan_in ** (-0.5)
        return {'x': jax.random.normal(ks[0], (B_, C_, H_, W_), jnp.float32), 'proj_w': rn(ks[1], (C_, C_), C_), 'in_proj_w': rn(ks[2], (2 * D_INNER, C_), C_), 'conv_w': rn(ks[3], (D_INNER, 1, D_CONV), D_CONV), 'conv_b': jax.random.normal(ks[4], (D_INNER,), jnp.float32) * 0.02, 'x_proj_w': rn(ks[5], (DT_RANK + 2 * D_STATE, D_INNER), D_INNER), 'dt_proj_w': rn(ks[6], (D_INNER, DT_RANK), DT_RANK), 'dt_proj_b': jax.random.normal(ks[7], (D_INNER,), jnp.float32) * 0.1, 'A_log': jax.random.uniform(ks[8], (D_INNER, D_STATE), jnp.float32), 'D': jax.random.normal(ks[9], (D_INNER,), jnp.float32), 'out_proj_w': rn(ks[10], (C_, D_INNER), D_INNER)}
    _L0_conv_all = _L0_conv_setup()
    _L0_conv_in = {k: v for k, v in _L0_conv_all.items() if k in ('proj_w', 'in_proj_w', 'conv_w', 'conv_b', 'x_proj_w', 'dt_proj_w', 'dt_proj_b', 'A_log', 'D', 'out_proj_w', )}
    del _L0_conv_all

    def _L1_conv_setup():
        import jax, jax.numpy as jnp
        import numpy as np
        UP, DOWN = (2, 2)
        PAD_LO, PAD_HI = (11, 10)
        FILTER_TAPS = 12
        N, C, H, W = (8, 128, 128, 128)
        TEMP_FS = 256.0
        CUTOFF, WIDTH = (64.0, 24.0)

        def _design_lowpass(numtaps, cutoff, width, fs):
            nyq = fs / 2.0
            atten = 2.285 * (numtaps - 1) * np.pi * (width / nyq) + 7.95
            if atten > 50:
                beta = 0.1102 * (atten - 8.7)
            elif atten > 21:
                beta = 0.5842 * (atten - 21) ** 0.4 + 0.07886 * (atten - 21)
            else:
                beta = 0.0
            m = np.arange(numtaps) - (numtaps - 1) / 2.0
            c = cutoff / nyq
            h = c * np.sinc(c * m) * np.kaiser(numtaps, beta)
            return (h / h.sum()).astype(np.float32)

        def _conv1d(x, k, axis, stride=1, dilation=1, pad=(0, 0)):
            n, c, h, w = x.shape
            xr = x.reshape(n * c, 1, h, w)
            if axis == 2:
                kern = k[::-1].reshape(1, 1, -1, 1)
                strides, ldil, padding = ((stride, 1), (dilation, 1), (tuple(pad), (0, 0)))
            else:
                kern = k[::-1].reshape(1, 1, 1, -1)
                strides, ldil, padding = ((1, stride), (1, dilation), ((0, 0), tuple(pad)))
            y = jax.lax.conv_general_dilated(xr, kern, window_strides=strides, padding=padding, lhs_dilation=ldil, dimension_numbers=('NCHW', 'OIHW', 'NCHW'))
            return y.reshape(n, c, y.shape[2], y.shape[3])
        key = jax.random.key(seed)
        kx, kb = jax.random.split(key)
        x = jax.random.normal(kx, (N, C, H, W), dtype=jnp.float32)
        b = jax.random.normal(kb, (C,), dtype=jnp.float32) * 0.1
        fu = jnp.asarray(_design_lowpass(FILTER_TAPS, CUTOFF, WIDTH, TEMP_FS))
        fd = jnp.asarray(_design_lowpass(FILTER_TAPS, CUTOFF, WIDTH, TEMP_FS))
        return {'x': x, 'b': b, 'up_filter': fu, 'down_filter': fd, 'gain': jnp.float32(np.sqrt(2.0)), 'slope': jnp.float32(0.2), 'clamp': jnp.float32(256.0)}
    _L1_conv_all = _L1_conv_setup()
    _L1_conv_in = {k: v for k, v in _L1_conv_all.items() if k in ('b', 'up_filter', 'down_filter', 'gain', 'slope', 'clamp', )}
    del _L1_conv_all

    def _L2_conv_setup():
        import jax, jax.numpy as jnp
        import numpy as np
        from jax import lax
        B, C, H, W, K = (32, 128, 56, 56, 5)
        CR = C // 4
        CE = 4 * C
        EPS = 1e-06

        def _ln(v, w, b, axis):
            u = v.mean(axis, keepdims=True)
            s2 = jnp.square(v - u).mean(axis, keepdims=True)
            return (v - u) * lax.rsqrt(s2 + EPS) * w + b
        key = jax.random.key(seed)
        ks = jax.random.split(key, 8)
        s = lambda fan: 1.0 / np.sqrt(fan)
        return {'x': jax.random.normal(ks[0], (B, C, H, W), jnp.float32), 'w_fc1': jax.random.normal(ks[1], (CR, C), jnp.float32) * s(C), 'ln1_w': jnp.ones((CR,), jnp.float32), 'ln1_b': jnp.zeros((CR,), jnp.float32), 'w_fc2': jax.random.normal(ks[2], (C * K * K, CR), jnp.float32) * s(CR), 'ln2_w': jnp.ones((C,), jnp.float32), 'ln2_b': jnp.zeros((C,), jnp.float32), 'w_expand': jax.random.normal(ks[3], (CE, C), jnp.float32) * s(C), 'w_shrink': jax.random.normal(ks[4], (C, CE), jnp.float32) * s(CE), 'grn_gamma': jax.random.normal(ks[5], (CE,), jnp.float32) * 0.1, 'grn_beta': jax.random.normal(ks[6], (CE,), jnp.float32) * 0.1}
    _L2_conv_all = _L2_conv_setup()
    _L2_conv_in = {k: v for k, v in _L2_conv_all.items() if k in ('w_fc1', 'ln1_w', 'ln1_b', 'w_fc2', 'ln2_w', 'ln2_b', 'w_expand', 'w_shrink', 'grn_gamma', 'grn_beta', )}
    del _L2_conv_all

    def _L3_conv_setup():
        import jax, jax.numpy as jnp
        import numpy as np
        N_GROUPS = 32
        N_HEADS = 4
        EPS = 1e-06
        B, C, H, W = (2, 128, 64, 64)

        def _rotary2d_pos(c, h, w):
            dh = c // 2
            inv_freq = 1.0 / 10000.0 ** (np.arange(0, dh, 2, dtype=np.float32) / dh)
            fh = np.arange(h, dtype=np.float32)[:, None] * inv_freq[None, :]
            fw = np.arange(w, dtype=np.float32)[:, None] * inv_freq[None, :]
            fh = np.broadcast_to(fh[:, None, :], (h, w, c // 4))
            fw = np.broadcast_to(fw[None, :, :], (h, w, c // 4))
            freqs = np.concatenate([fh, fw], axis=-1).reshape(h * w, dh)
            return jnp.asarray(np.concatenate([np.sin(freqs), np.cos(freqs)], axis=-1))

        def _apply_rotary(pos, t):
            sin, cos = jnp.split(pos, 2, axis=-1)
            sin_pos = jnp.stack([sin, sin], axis=-1).reshape(pos.shape)
            cos_pos = jnp.stack([cos, cos], axis=-1).reshape(pos.shape)
            t2 = jnp.stack([-t[..., 1::2], t[..., ::2]], axis=-1).reshape(t.shape)
            return t * cos_pos + t2 * sin_pos
        key = jax.random.key(seed)
        ks = jax.random.split(key, 7)
        x = jax.random.normal(ks[0], (B, C, H, W), dtype=jnp.float32)
        gn_w = 1.0 + 0.1 * jax.random.normal(ks[1], (C,), dtype=jnp.float32)
        gn_b = 0.1 * jax.random.normal(ks[2], (C,), dtype=jnp.float32)
        w_qkv = 0.02 * jax.random.normal(ks[3], (3 * C, C), dtype=jnp.float32)
        b_qkv = 0.02 * jax.random.normal(ks[4], (3 * C,), dtype=jnp.float32)
        w_proj = 0.02 * jax.random.normal(ks[5], (C, C), dtype=jnp.float32)
        b_proj = 0.02 * jax.random.normal(ks[6], (C,), dtype=jnp.float32)
        return {'x': x, 'gn_w': gn_w, 'gn_b': gn_b, 'w_qkv': w_qkv, 'b_qkv': b_qkv, 'w_proj': w_proj, 'b_proj': b_proj}
    _L3_conv_all = _L3_conv_setup()
    _L3_conv_in = {k: v for k, v in _L3_conv_all.items() if k in ('gn_w', 'gn_b', 'w_qkv', 'b_qkv', 'w_proj', 'b_proj', )}
    del _L3_conv_all

    return {
        "x": x,
        "L0_conv_proj_w": _L0_conv_in["proj_w"],
        "L0_conv_in_proj_w": _L0_conv_in["in_proj_w"],
        "L0_conv_conv_w": _L0_conv_in["conv_w"],
        "L0_conv_conv_b": _L0_conv_in["conv_b"],
        "L0_conv_x_proj_w": _L0_conv_in["x_proj_w"],
        "L0_conv_dt_proj_w": _L0_conv_in["dt_proj_w"],
        "L0_conv_dt_proj_b": _L0_conv_in["dt_proj_b"],
        "L0_conv_A_log": _L0_conv_in["A_log"],
        "L0_conv_D": _L0_conv_in["D"],
        "L0_conv_out_proj_w": _L0_conv_in["out_proj_w"],
        "L1_conv_b": _L1_conv_in["b"],
        "L1_conv_up_filter": _L1_conv_in["up_filter"],
        "L1_conv_down_filter": _L1_conv_in["down_filter"],
        "L1_conv_gain": _L1_conv_in["gain"],
        "L1_conv_slope": _L1_conv_in["slope"],
        "L1_conv_clamp": _L1_conv_in["clamp"],
        "L2_conv_w_fc1": _L2_conv_in["w_fc1"],
        "L2_conv_ln1_w": _L2_conv_in["ln1_w"],
        "L2_conv_ln1_b": _L2_conv_in["ln1_b"],
        "L2_conv_w_fc2": _L2_conv_in["w_fc2"],
        "L2_conv_ln2_w": _L2_conv_in["ln2_w"],
        "L2_conv_ln2_b": _L2_conv_in["ln2_b"],
        "L2_conv_w_expand": _L2_conv_in["w_expand"],
        "L2_conv_w_shrink": _L2_conv_in["w_shrink"],
        "L2_conv_grn_gamma": _L2_conv_in["grn_gamma"],
        "L2_conv_grn_beta": _L2_conv_in["grn_beta"],
        "L3_conv_gn_w": _L3_conv_in["gn_w"],
        "L3_conv_gn_b": _L3_conv_in["gn_b"],
        "L3_conv_w_qkv": _L3_conv_in["w_qkv"],
        "L3_conv_b_qkv": _L3_conv_in["b_qkv"],
        "L3_conv_w_proj": _L3_conv_in["w_proj"],
        "L3_conv_b_proj": _L3_conv_in["b_proj"],
    }

def reference(x, L0_conv_proj_w, L0_conv_in_proj_w, L0_conv_conv_w, L0_conv_conv_b, L0_conv_x_proj_w, L0_conv_dt_proj_w, L0_conv_dt_proj_b, L0_conv_A_log, L0_conv_D, L0_conv_out_proj_w, L1_conv_b, L1_conv_up_filter, L1_conv_down_filter, L1_conv_gain, L1_conv_slope, L1_conv_clamp, L2_conv_w_fc1, L2_conv_ln1_w, L2_conv_ln1_b, L2_conv_w_fc2, L2_conv_ln2_w, L2_conv_ln2_b, L2_conv_w_expand, L2_conv_w_shrink, L2_conv_grn_gamma, L2_conv_grn_beta, L3_conv_gn_w, L3_conv_gn_b, L3_conv_w_qkv, L3_conv_b_qkv, L3_conv_w_proj, L3_conv_b_proj):
    import jax
    import jax.numpy as jnp
    def _L0_conv_ref(x, proj_w, in_proj_w, conv_w, conv_b, x_proj_w, dt_proj_w, dt_proj_b, A_log, D, out_proj_w):
        import jax, jax.numpy as jnp
        import numpy as np
        from jax import lax
        B_, C_, H_, W_ = (4, 128, 64, 64)
        D_INNER, D_STATE, DT_RANK, D_CONV = (256, 16, 8, 4)

        def _mamba2d(x, proj_w, in_proj_w, conv_w, conv_b, x_proj_w, dt_proj_w, dt_proj_b, A_log, D, out_proj_w):
            b, c, h, w = x.shape
            L = h * w
            u = jnp.einsum('oc,bchw->bohw', proj_w, x).reshape(b, c, L).transpose(0, 2, 1)
            xz = u @ in_proj_w.T
            xs, zg = (xz[..., :D_INNER], xz[..., D_INNER:])
            xt = xs.transpose(0, 2, 1)
            xt = lax.conv_general_dilated(xt, conv_w, window_strides=(1,), padding=[(D_CONV - 1, 0)], feature_group_count=D_INNER)
            xc = jax.nn.silu(xt + conv_b[None, :, None]).transpose(0, 2, 1)
            x_dbl = xc @ x_proj_w.T
            dt_r = x_dbl[..., :DT_RANK]
            Bm = x_dbl[..., DT_RANK:DT_RANK + D_STATE]
            Cm = x_dbl[..., DT_RANK + D_STATE:]
            delta = jax.nn.softplus(dt_r @ dt_proj_w.T + dt_proj_b)
            A = -jnp.exp(A_log)

            def step(hprev, inp):
                dt_t, B_t, C_t, x_t = inp
                dA = jnp.exp(dt_t[:, :, None] * A)
                hn = dA * hprev + (dt_t * x_t)[:, :, None] * B_t[:, None, :]
                y = jnp.einsum('bdn,bn->bd', hn, C_t)
                return (hn, y)
            h0 = jnp.zeros((b, D_INNER, D_STATE), xc.dtype)
            _, ys = lax.scan(step, h0, (delta.transpose(1, 0, 2), Bm.transpose(1, 0, 2), Cm.transpose(1, 0, 2), xc.transpose(1, 0, 2)))
            y = ys.transpose(1, 0, 2) + xc * D
            y = y * jax.nn.silu(zg)
            out = y @ out_proj_w.T
            return out.transpose(0, 2, 1).reshape(b, c, h, w) + x
        return _mamba2d(x, proj_w, in_proj_w, conv_w, conv_b, x_proj_w, dt_proj_w, dt_proj_b, A_log, D, out_proj_w)

    def _L1_conv_ref(x, b, up_filter, down_filter, gain, slope, clamp):
        import jax, jax.numpy as jnp
        import numpy as np
        UP, DOWN = (2, 2)
        PAD_LO, PAD_HI = (11, 10)
        FILTER_TAPS = 12
        N, C, H, W = (8, 128, 128, 128)
        TEMP_FS = 256.0
        CUTOFF, WIDTH = (64.0, 24.0)

        def _design_lowpass(numtaps, cutoff, width, fs):
            nyq = fs / 2.0
            atten = 2.285 * (numtaps - 1) * np.pi * (width / nyq) + 7.95
            if atten > 50:
                beta = 0.1102 * (atten - 8.7)
            elif atten > 21:
                beta = 0.5842 * (atten - 21) ** 0.4 + 0.07886 * (atten - 21)
            else:
                beta = 0.0
            m = np.arange(numtaps) - (numtaps - 1) / 2.0
            c = cutoff / nyq
            h = c * np.sinc(c * m) * np.kaiser(numtaps, beta)
            return (h / h.sum()).astype(np.float32)

        def _conv1d(x, k, axis, stride=1, dilation=1, pad=(0, 0)):
            n, c, h, w = x.shape
            xr = x.reshape(n * c, 1, h, w)
            if axis == 2:
                kern = k[::-1].reshape(1, 1, -1, 1)
                strides, ldil, padding = ((stride, 1), (dilation, 1), (tuple(pad), (0, 0)))
            else:
                kern = k[::-1].reshape(1, 1, 1, -1)
                strides, ldil, padding = ((1, stride), (1, dilation), ((0, 0), tuple(pad)))
            y = jax.lax.conv_general_dilated(xr, kern, window_strides=strides, padding=padding, lhs_dilation=ldil, dimension_numbers=('NCHW', 'OIHW', 'NCHW'))
            return y.reshape(n, c, y.shape[2], y.shape[3])
        x = x + b[None, :, None, None]
        fu = up_filter * UP
        x = _conv1d(x, fu, axis=2, dilation=UP, pad=(PAD_LO, PAD_HI + UP - 1))
        x = _conv1d(x, fu, axis=3, dilation=UP, pad=(PAD_LO, PAD_HI + UP - 1))
        x = jnp.where(x >= 0, x, x * slope) * gain
        x = jnp.clip(x, -clamp, clamp)
        x = _conv1d(x, down_filter, axis=2, stride=DOWN)
        x = _conv1d(x, down_filter, axis=3, stride=DOWN)
        return x

    def _L2_conv_ref(x, w_fc1, ln1_w, ln1_b, w_fc2, ln2_w, ln2_b, w_expand, w_shrink, grn_gamma, grn_beta):
        import jax, jax.numpy as jnp
        import numpy as np
        from jax import lax
        B, C, H, W, K = (32, 128, 56, 56, 5)
        CR = C // 4
        CE = 4 * C
        EPS = 1e-06

        def _ln(v, w, b, axis):
            u = v.mean(axis, keepdims=True)
            s2 = jnp.square(v - u).mean(axis, keepdims=True)
            return (v - u) * lax.rsqrt(s2 + EPS) * w + b
        b, c, h, w = x.shape
        pooled = x.mean((2, 3))
        hdn = pooled @ w_fc1.T
        hdn = _ln(hdn, ln1_w, ln1_b, axis=-1)
        dyn = hdn @ w_fc2.T
        dyn_w = dyn.reshape(b * c, 1, K, K)
        pad = K // 2
        out = lax.conv_general_dilated(x.reshape(1, b * c, h, w), dyn_w, window_strides=(1, 1), padding=[(pad, pad), (pad, pad)], dimension_numbers=('NCHW', 'OIHW', 'NCHW'), feature_group_count=b * c).reshape(b, c, h, w)
        u = out.mean(1, keepdims=True)
        s2 = jnp.square(out - u).mean(1, keepdims=True)
        out = (out - u) * lax.rsqrt(s2 + EPS)
        out = ln2_w[None, :, None, None] * out + ln2_b[None, :, None, None]
        out = jnp.einsum('bchw,oc->bohw', out, w_expand)
        out = jax.nn.gelu(out, approximate=False)
        gx = jnp.sqrt(jnp.sum(jnp.square(out), axis=(2, 3), keepdims=True))
        nx = gx / (gx.mean(1, keepdims=True) + EPS)
        g = grn_gamma[None, :, None, None]
        bt = grn_beta[None, :, None, None]
        out = g * (out * nx) + bt + out
        out = jnp.einsum('bohw,co->bchw', out, w_shrink)
        return out + x

    def _L3_conv_ref(x, gn_w, gn_b, w_qkv, b_qkv, w_proj, b_proj):
        import jax, jax.numpy as jnp
        import numpy as np
        N_GROUPS = 32
        N_HEADS = 4
        EPS = 1e-06
        B, C, H, W = (2, 128, 64, 64)

        def _rotary2d_pos(c, h, w):
            dh = c // 2
            inv_freq = 1.0 / 10000.0 ** (np.arange(0, dh, 2, dtype=np.float32) / dh)
            fh = np.arange(h, dtype=np.float32)[:, None] * inv_freq[None, :]
            fw = np.arange(w, dtype=np.float32)[:, None] * inv_freq[None, :]
            fh = np.broadcast_to(fh[:, None, :], (h, w, c // 4))
            fw = np.broadcast_to(fw[None, :, :], (h, w, c // 4))
            freqs = np.concatenate([fh, fw], axis=-1).reshape(h * w, dh)
            return jnp.asarray(np.concatenate([np.sin(freqs), np.cos(freqs)], axis=-1))

        def _apply_rotary(pos, t):
            sin, cos = jnp.split(pos, 2, axis=-1)
            sin_pos = jnp.stack([sin, sin], axis=-1).reshape(pos.shape)
            cos_pos = jnp.stack([cos, cos], axis=-1).reshape(pos.shape)
            t2 = jnp.stack([-t[..., 1::2], t[..., ::2]], axis=-1).reshape(t.shape)
            return t * cos_pos + t2 * sin_pos
        b, c, h, w = x.shape
        L = h * w
        xg = jnp.transpose(x, (0, 2, 3, 1)).reshape(b, h, w, N_GROUPS, c // N_GROUPS)
        mean = jnp.mean(xg, axis=(1, 2, 3), keepdims=True)
        var = jnp.var(xg, axis=(1, 2, 3), keepdims=True, ddof=1)
        xn = (xg - mean) * jax.lax.rsqrt(var + EPS)
        xn = xn.reshape(b, h, w, c) * gn_w + gn_b
        xn = jnp.transpose(xn, (0, 3, 1, 2))
        xi = xn.reshape(b, c, L)
        qkv = jnp.einsum('oc,bcl->bol', w_qkv, xi) + b_qkv[None, :, None]
        q, k, v = jnp.split(jnp.transpose(qkv, (0, 2, 1)), 3, axis=2)
        pos = _rotary2d_pos(c, h, w)
        q = _apply_rotary(pos, q)
        k = _apply_rotary(pos, k)
        ch = c // N_HEADS
        scale = 1.0 / np.sqrt(np.sqrt(ch))
        qh = jnp.transpose(q, (0, 2, 1)).reshape(b * N_HEADS, ch, L)
        kh = jnp.transpose(k, (0, 2, 1)).reshape(b * N_HEADS, ch, L)
        vh = jnp.transpose(v, (0, 2, 1)).reshape(b * N_HEADS, ch, L)
        weight = jnp.einsum('bct,bcs->bts', qh * scale, kh * scale)
        weight = jax.nn.softmax(weight.astype(jnp.float16), axis=-1).astype(weight.dtype)
        a = jnp.einsum('bts,bcs->bct', weight, vh).reshape(b, c, L)
        hout = jnp.einsum('oc,bcl->bol', w_proj, a) + b_proj[None, :, None]
        return (xi + hout).reshape(b, c, h, w)

    def _gn(v, G=32, eps=1e-5):
        B_, C_, H_, W_ = v.shape
        g = v.reshape(B_, G, C_ // G, H_, W_)
        m = jnp.mean(g, axis=(2, 3, 4), keepdims=True)
        s = jnp.var(g, axis=(2, 3, 4), keepdims=True)
        return ((g - m) / jnp.sqrt(s + eps)).reshape(v.shape)

    def _ln_c(v, eps=1e-6):
        m = jnp.mean(v, axis=1, keepdims=True)
        s = jnp.var(v, axis=1, keepdims=True)
        return (v - m) / jnp.sqrt(s + eps)

    def _ln_t(v, eps=1e-5):
        m = jnp.mean(v, axis=-1, keepdims=True)
        s = jnp.var(v, axis=-1, keepdims=True)
        return (v - m) / jnp.sqrt(s + eps)

    def _to_tokens(v):
        B_, C_, H_, W_ = v.shape
        return v.reshape(B_, C_, H_ * W_).transpose(0, 2, 1)
    def _from_tokens(t, like):
        B_, C_, H_, W_ = like.shape
        return t.transpose(0, 2, 1).reshape(B_, C_, H_, W_)

    x = _L0_conv_ref(x, L0_conv_proj_w, L0_conv_in_proj_w, L0_conv_conv_w, L0_conv_conv_b, L0_conv_x_proj_w, L0_conv_dt_proj_w, L0_conv_dt_proj_b, L0_conv_A_log, L0_conv_D, L0_conv_out_proj_w)
    x = _L1_conv_ref(x, L1_conv_b, L1_conv_up_filter, L1_conv_down_filter, L1_conv_gain, L1_conv_slope, L1_conv_clamp)
    x = _L2_conv_ref(x, L2_conv_w_fc1, L2_conv_ln1_w, L2_conv_ln1_b, L2_conv_w_fc2, L2_conv_ln2_w, L2_conv_ln2_b, L2_conv_w_expand, L2_conv_w_shrink, L2_conv_grn_gamma, L2_conv_grn_beta)
    x = _L3_conv_ref(x, L3_conv_gn_w, L3_conv_gn_b, L3_conv_w_qkv, L3_conv_b_qkv, L3_conv_w_proj, L3_conv_b_proj)
    return x


_drawn_inputs = setup_inputs


def setup_inputs(seed=0):
    import zlib

    import numpy as np

    out = dict(_drawn_inputs(seed))
    spreads = {'L2_conv_ln1_w': (1.0, 0.2),
     'L2_conv_ln1_b': (0.0, 0.1),
     'L2_conv_ln2_w': (1.0, 0.2),
     'L2_conv_ln2_b': (0.0, 0.1)}
    factors = {'L0_conv_conv_b': 3.391,
     'L3_conv_w_qkv': 2.955,
     'L3_conv_b_qkv': 8.0,
     'L3_conv_w_proj': 3.179,
     'L3_conv_b_proj': 2.716}
    for name, (base, spread) in spreads.items():
        noise = np.random.default_rng([zlib.crc32(name.encode()), seed]).standard_normal(out[name].shape)
        drawn = base * np.exp(spread * noise) if base else spread * noise
        out[name] = jnp.asarray(drawn.astype(out[name].dtype))
    for name, factor in factors.items():
        out[name] = (out[name] * factor).astype(out[name].dtype)
    return out
```

```python
from contextlib import ExitStack

import numpy as np

import concourse.bass as bass
from concourse import mybir


def mamba_phase(nc, x_in, proj_w, in_projT, conv_wT, conv_b, x_proj_cols, dt_projT, dt_b, A_log, D, out_projT,
                next_bias, ident, row_select, out):
    f32, bf16 = mybir.dt.float32, mybir.dt.bfloat16
    ALU, ACT = mybir.AluOpType, mybir.ActivationFunctionType
    BATCH, C, L = x_in.shape
    INNER = in_projT.shape[1] // 2
    DT = INNER // 128
    STATES = A_log.shape[2]
    RANK = dt_projT.shape[0]
    CONV = conv_wT.shape[0]
    T = 512
    CHUNKS = L // T
    BC = 2 * STATES
    HALO = CONV - 1
    XLEN = HALO + L
    DTR = 3 * BC

    with ExitStack() as ctx:
        def sb(name, shape, dt=f32):
            return ctx.enter_context(nc.sbuf_tensor("mb_" + name, shape, dt))

        def ps(name, shape):
            return ctx.enter_context(nc.psum_tensor("mb_" + name, shape, f32))

        def sem(name):
            return ctx.enter_context(nc.semaphore("mb_" + name))

        x_sb = sb("x", [C, 2 * XLEN])
        proj_sb, inT = sb("proj", [C, C]), sb("inT", [C, 2 * INNER])
        taps_row = sb("taps_row", [C, CONV, INNER])
        wT = sb("wT", [C, 2 * INNER])
        tapT = sb("tapT", [C, CONV, INNER])
        xprojT = sb("xprojT", [128, DT, DTR + RANK])
        dtT = sb("dtT", [DTR + RANK, INNER])
        outT = sb("outT", [128, DT, C])
        cb, db, Dv = sb("cb", [128, DT]), sb("db", [128, DT]), sb("Dv", [128, DT])
        nb = sb("nb", [C, 1])
        A_sb = sb("A", [128, DT, STATES])
        ident_sb = sb("ident", [128, 128])
        pick32, pick = sb("pick32", [DTR, BC]), sb("pick", [DTR, BC, 128], bf16)
        conv_out = sb("conv_out", [128, 2, DT, T])
        gate = sb("gate", [128, 2, DT, T])
        bc_parts = sb("bc_parts", [DTR, 2, T], bf16)
        remainder = sb("remainder", [DTR, T])
        middle = sb("middle", [DTR, T], bf16)
        rank_rows = sb("rank_rows", [DTR + RANK, T])
        sp_log, sp_max = sb("sp_log", [128, DT, T]), sb("sp_max", [128, DT, T])
        delta, du = sb("delta", [128, 2, DT, T]), sb("du", [128, 2, DT, T])
        decay = sb("decay", [128, 2, DT, T])
        drive = sb("drive", [128, 2, DT, T])
        c_sb = sb("c_row", [128, 2, T])
        weighted = sb("weighted", [128, 2, DT, T])
        states = sb("states", [128, DT, STATES, T])
        carry = sb("carry", [128, DT, STATES])
        skip = sb("skip", [128, DT, T])
        outbuf = sb("outbuf", [C, T])

        y_ps = ps("y", [128, DT, T])
        b_ps = ps("b", [128, 2, T])
        c_ps = ps("c", [128, 2, T])
        front_ps = ps("front", [128, 2, T])

        consts_in, halo_made, setup_ps = sem("consts_in"), sem("halo_made"), sem("setup_ps")
        setup_act, setup_dve = sem("setup_act"), sem("setup_dve")
        x_loaded, stored = sem("x_loaded"), sem("stored")
        conv_ps, conv_ready, gate_ps, gate_ready = sem("conv_ps"), sem("conv_ready"), sem("gate_ps"), sem("gate_ready")
        bc_ps, high_ready, rank_ready = sem("bc_ps"), sem("high_ready"), sem("rank_ready")
        remainder_ready, middle_ready, parts_ready = sem("remainder_ready"), sem("middle_ready"), sem("parts_ready")
        low_ready = sem("low_ready")
        dt_ps, abs_ready, exp_ready, log_ready = sem("dt_ps"), sem("abs_ready"), sem("exp_ready"), sem("log_ready")
        max_ready, delta_ready, du_ready = sem("max_ready"), sem("delta_ready"), sem("du_ready")
        rows_filled = sem("rows_filled")
        decay_ready = sem("decay_ready")
        drive_ready, c_ready, scanned, weighted_ready, summed = (
            sem("drive_ready"), sem("c_ready"), sem("scanned"), sem("weighted_ready"), sem("summed"))
        carried = sem("carried")
        skip_ready, gated_ready, out_ps, out_ready = sem("skip_ready"), sem("gated_ready"), sem("out_ps"), sem("out_ready")
        block = ctx.enter_context(nc.Block())

        def chunk_pairs(engine, body, start):
            start(0, True)
            body(0, 0, True, False)
            with engine.Fori(1, CHUNKS // 2) as half:
                body(0, half * 2, False, False)
            with engine.Fori(1, BATCH - 1) as b:
                start(b, True)
                with engine.Fori(0, CHUNKS // 2) as half:
                    body(b, half * 2, False, False)
            start(BATCH - 1, False)
            with engine.Fori(0, CHUNKS // 2 - 1) as half:
                body(BATCH - 1, half * 2, False, False)
            body(BATCH - 1, CHUNKS - 2, False, True)

        SKIP_AT, GATE_AT, PROJECT_AT, FINISH_AT = 0, 0, 3, 4
        SILU_AT, BC_AT, HIGH_AT, MIDDLE_AT, DT_AT, SOFTPLUS_AT, DELTA_AT, DU_AT, CONV_AT = 1, 2, 3, 4, 5, 6, 8, 10, 7

        def nothing(b, more):
            pass

        @block.sync
        def _(sp):
            for dst, src in [(proj_sb[:, :], proj_w), (inT[:, :], in_projT),
                             (taps_row[:, :, :], conv_wT.rearrange("(o k) d -> o k d", o=1).broadcast_to([C, CONV, INNER])),
                             (xprojT[:, :, :], x_proj_cols.rearrange("(t p) m -> p t m", t=DT)),
                             (dtT[DTR:DTR + RANK, :], dt_projT), (outT[:, :, :], out_projT.rearrange("(t p) c -> p t c", t=DT)),
                             (cb[:, :], conv_b), (db[:, :], dt_b), (Dv[:, :], D), (nb[:, :], next_bias),
                             (A_sb[:, :, :], A_log), (ident_sb[:, :], ident), (pick32[:, :], row_select)]:
                sp.dma_start(dst, src).then_inc(consts_in, 16)
            sp.wait_ge(halo_made, 4)

            def load(b):
                sp.dma_start(x_sb[:, bass.ds((b % 2) * XLEN + HALO, L)],
                             x_in[bass.ds(b, 1), :, :].rearrange("o c l -> (o c) l")).then_inc(x_loaded, 16)

            load(0)
            sp.wait_ge(x_loaded, 16)

            def start(b, more):
                if more:
                    sp.wait_ge(out_ready, b * CHUNKS)
                    load(b + 1)

            def body(b, c, first, last):
                for par in range(2):
                    k = b * CHUNKS + c + par
                    sp.wait_ge(out_ready, k + 1)
                    sp.dma_start(out[bass.ds(b, 1), :, bass.ds((c + par) * T, T)].rearrange("o c l -> (o c) l"),
                                 outbuf[:, :]).then_inc(stored, 16)

            chunk_pairs(sp, body, start)
            sp.wait_ge(stored, 16 * BATCH * CHUNKS)

        @block.gpsimd
        def _(pool):
            pool.memset(x_sb[:, 0:HALO], 0.0).then_inc(halo_made, 1)
            pool.memset(x_sb[:, XLEN:XLEN + HALO], 0.0).then_inc(halo_made, 1)
            pool.memset(dtT[0:DTR, :], 0.0).then_inc(halo_made, 1)
            pool.memset(rank_rows[0:DTR, :], 0.0).then_inc(halo_made, 1)

            def softplus_sum(k, par):
                for dt in range(DT):
                    pool.wait_ge(max_ready, k * DT + dt + 1)
                    pool.wait_ge(log_ready, k * DT + dt + 1)
                    pool.tensor_tensor(delta[:, par, dt, :], sp_max[:, dt, :], sp_log[:, dt, :],
                                       ALU.add).then_inc(delta_ready, 1)

            def apply_gate(k, par):
                for dt in range(DT):
                    pool.wait_ge(skip_ready, k * DT + dt + 1)
                    pool.wait_ge(gate_ready, k * DT + dt + 1)
                    pool.tensor_tensor(skip[:, dt, :], skip[:, dt, :], gate[:, par, dt, :],
                                       ALU.mult).then_inc(gated_ready, 1)

            softplus_sum(0, 0)

            def body(b, c, first, last):
                for par in range(2):
                    k = b * CHUNKS + c + par
                    for n in range(STATES):
                        s = k * STATES + n
                        for dt in range(DT):
                            pool.wait_ge(c_ready, s + 3)
                            pool.wait_ge(summed, s * DT + dt + 1)
                            pool.wait_ge(scanned, s * DT + dt + 5)
                            pool.tensor_tensor(weighted[:, n % 2, dt, :], states[:, dt, n, :], c_sb[:, n % 2, :],
                                               ALU.mult).then_inc(weighted_ready, 1)
                        if n == DELTA_AT and not (last and par == 1):
                            softplus_sum(k + 1, 1 - par)
                        if n == GATE_AT and not (first and par == 0):
                            apply_gate(k - 1, 1 - par)
            
            chunk_pairs(pool, body, nothing)
            apply_gate(BATCH * CHUNKS - 1, 1)

        @block.scalar
        def _(act):
            act.wait_ge(consts_in, 16 * 13)
            act.wait_ge(setup_ps, 1)
            act.activation(wT[:, :], front_ps[:, 0, :], ACT.Copy).then_inc(setup_act, 1)
            act.activation(A_sb[:, :, :], A_sb[:, :, :], ACT.Exp).then_inc(setup_act, 1)
            act.activation(pick[:, :, :], pick32[:, :].rearrange("p (n o) -> p n o", o=1).broadcast_to([DTR, BC, 128]),
                           ACT.Copy).then_inc(setup_act, 1)
            act.wait_ge(setup_dve, 2)

            def take_conv(k, par, dt, early):
                act.wait_ge(conv_ps, k * DT + dt + 1)
                if early is False:
                    act.wait_ge(skip_ready, (k - 1) * DT)
                act.activation(conv_out[:, par, dt, :], front_ps[:, dt, :], ACT.Silu,
                               bias=cb[:, dt:dt + 1]).then_inc(conv_ready, 1)

            def take_gate(k, par, dt, early):
                act.wait_ge(gate_ps, k * DT + dt + 1)
                if early is False:
                    act.wait_ge(gated_ready, (k - 1) * DT)
                act.activation(gate[:, par, dt, :], front_ps[:, dt, :], ACT.Silu).then_inc(gate_ready, 1)

            def take_high(k, par):
                act.wait_ge(bc_ps, k + 1)
                act.activation(bc_parts[:, par, :], front_ps[0:DTR, 0, :], ACT.Copy).then_inc(high_ready, 1)
                act.activation(rank_rows[DTR:DTR + RANK, :], front_ps[DTR:DTR + RANK, 0, :], ACT.Copy).then_inc(rank_ready, 1)

            def take_middle(k, par):
                act.wait_ge(remainder_ready, k + 1)
                act.activation(middle[:, :], remainder[:, :], ACT.Copy).then_inc(middle_ready, 1)
                act.activation(bc_parts[BC:2 * BC, par, :], remainder[BC:2 * BC, :], ACT.Copy).then_inc(parts_ready, 1)

            def softplus_log(k):
                for dt in range(DT):
                    act.wait_ge(dt_ps, k * DT + dt + 1)
                    act.wait_ge(delta_ready, k * DT)
                    act.activation(sp_log[:, dt, :], front_ps[:, 1 - dt, :], ACT.Abs, bias=db[:, dt:dt + 1]).then_inc(abs_ready, 1)
                for dt in range(DT):
                    act.wait_ge(abs_ready, k * DT + dt + 1)
                    act.activation(sp_log[:, dt, :], sp_log[:, dt, :], ACT.Exp, scale=-1.0).then_inc(exp_ready, 1)
                for dt in range(DT):
                    act.wait_ge(exp_ready, k * DT + dt + 1)
                    act.activation(sp_log[:, dt, :], sp_log[:, dt, :], ACT.Ln, bias=1.0).then_inc(log_ready, 1)

            def state_inputs(k, par, n):
                s = k * STATES + n
                for dt in range(DT):
                    act.wait_ge(delta_ready, k * DT + dt + 1)
                    act.wait_ge(scanned, s * DT + dt + 1)
                    act.activation(decay[:, n % 2, dt, :], delta[:, par, dt, :], ACT.Exp,
                                   scale=A_sb[:, dt, n:n + 1]).then_inc(decay_ready, 1)
                act.wait_ge(rows_filled, s + 1)
                act.wait_ge(weighted_ready, s * DT + 2)
                act.activation(c_sb[:, n % 2, :], c_ps[:, n % 2, :], ACT.Copy).then_inc(c_ready, 1)

            def front_step(k, par, n, early):
                if n == SILU_AT:
                    for dt in range(DT):
                        take_conv(k, par, dt, early)
                    for dt in range(DT):
                        take_gate(k, par, dt, early)
                    act.preload_act_table_set("natural_log_exp_and_others")
                if n == HIGH_AT:
                    take_high(k, par)
                if n == MIDDLE_AT:
                    take_middle(k, par)
                if n == SOFTPLUS_AT:
                    softplus_log(k)

            for n in range(STATES):
                front_step(0, 0, n, True)
            state_inputs(0, 0, 0)

            def body(b, c, first, last):
                for par in range(2):
                    k = b * CHUNKS + c + par
                    final = last and par == 1
                    for n in range(STATES):
                        if n + 1 < STATES:
                            state_inputs(k, par, n + 1)
                        elif not final:
                            state_inputs(k + 1, 1 - par, 0)
                        if not final:
                            front_step(k + 1, 1 - par, n, first and par == 0)

            chunk_pairs(act, body, nothing)

        @block.tensor
        def _(pe):
            pe.sem_inc(drive_ready, 4)
            pe.sem_inc(scanned, 4)
            pe.sem_inc(weighted_ready, 4)
            pe.sem_inc(summed, 4)
            pe.sem_inc(c_ready, 2)
            pe.wait_ge(consts_in, 16 * 13)
            pe.matmul(front_ps[:, 0, :], proj_sb[:, :], inT[:, :], start=True, stop=True).then_inc(setup_ps, 1)
            pe.wait_ge(setup_act, 3)
            pe.wait_ge(setup_dve, 2)

            def conv(b, c, k, step):
                dt, j = divmod(step, CONV)
                if step == 0:
                    pe.wait_ge(max_ready, k * DT)
                    pe.wait_ge(x_loaded, b * 16 + 16)
                last = pe.matmul(front_ps[:, dt, :], tapT[:, j, dt * 128:(dt + 1) * 128],
                                 x_sb[:, bass.ds((b % 2) * XLEN + c * T + j, T)], start=j == 0, stop=j == CONV - 1)
                if j == CONV - 1:
                    last.then_inc(conv_ps, 1)

            def gates(b, c, k):
                for dt in range(DT):
                    pe.wait_ge(conv_ready, k * DT + dt + 1)
                    pe.matmul(front_ps[:, dt, :], wT[:, INNER + dt * 128:INNER + (dt + 1) * 128],
                              x_sb[:, bass.ds((b % 2) * XLEN + c * T + HALO, T)], start=True, stop=True).then_inc(gate_ps, 1)

            def bc_rows(k, par):
                pe.wait_ge(conv_ready, (k + 1) * DT)
                pe.wait_ge(gate_ready, k * DT + 1)
                for dt in range(DT):
                    last = pe.matmul(front_ps[0:DTR + RANK, 0, :], xprojT[:, dt, :], conv_out[:, par, dt, :],
                                     start=dt == 0, stop=dt == DT - 1)
                last.then_inc(bc_ps, 1)

            def dt_rows(k, early):
                pe.wait_ge(rank_ready, k + 1)
                if not early:
                    pe.wait_ge(out_ready, k - 1)
                for dt in range(DT):
                    if dt == 0:
                        pe.wait_ge(gate_ready, (k + 1) * DT)
                    else:
                        pe.wait_ge(remainder_ready, k + 1)
                    pe.matmul(front_ps[:, 1 - dt, :], dtT[:, dt * 128:(dt + 1) * 128],
                              rank_rows[:, :], start=True, stop=True).then_inc(dt_ps, 1)

            def project(k, ends):
                pe.wait_ge(gated_ready, (k + 1) * DT)
                if not ends:
                    pe.wait_ge(gate_ready, (k + 3) * DT)
                else:
                    pe.wait_ge(max_ready, (k + 1) * DT)
                for dt in range(DT):
                    last = pe.matmul(front_ps[:, 1, :], outT[:, dt, :], skip[:, dt, :], start=dt == 0, stop=dt == DT - 1)
                last.then_inc(out_ps, 1)

            def rows(k, par, n):
                s = k * STATES + n
                if n == 0:
                    pe.wait_ge(parts_ready, k + 1)
                    pe.wait_ge(low_ready, k + 1)
                pe.wait_ge(drive_ready, s * DT + 2)
                pe.wait_ge(c_ready, s + 1)
                pe.matmul(b_ps[:, n % 2, :], pick[:, n, :], bc_parts[:, par, :], start=True, stop=True)
                pe.matmul(c_ps[:, n % 2, :], pick[:, STATES + n, :], bc_parts[:, par, :], start=True,
                          stop=True).then_inc(rows_filled, 1)

            def sum_states(k, n):
                s = k * STATES + n
                if n == 0:
                    pe.wait_ge(skip_ready, k * DT)
                for dt in range(DT):
                    pe.wait_ge(weighted_ready, s * DT + dt + 5)
                    pe.matmul(y_ps[:, dt, :], ident_sb[:, :], weighted[:, n % 2, dt, :], start=n == 0,
                              stop=n == STATES - 1).then_inc(summed, 1)

            def front_step(b, c, k, par, n, early):
                if n == BC_AT:
                    bc_rows(k, par)
                if n == DT_AT:
                    dt_rows(k, early)

            for step in range(DT * CONV):
                conv(0, 0, 0, step)
            for n in range(STATES):
                front_step(0, 0, 0, 0, n, True)
                if n == SILU_AT:
                    gates(0, 0, 0)
            for step in range(DT * CONV):
                conv(0, 1, 1, step)
            rows(0, 0, 0)

            def body(b, c, first, last):
                for par in range(2):
                    k = b * CHUNKS + c + par
                    final = last and par == 1
                    k1 = k + 1
                    b1, c1 = (k1 // CHUNKS, k1 % CHUNKS)
                    for n in range(STATES):
                        if n + 1 < STATES:
                            rows(k, par, n + 1)
                        elif not final:
                            rows(k + 1, 1 - par, 0)
                        if not final:
                            front_step(b1, c1, k + 1, 1 - par, n, first and par == 0)
                        if n:
                            sum_states(k, n - 1)
                        if n == SILU_AT and not final:
                            gates(b1, c1, k + 1)
                        if CONV_AT <= n < CONV_AT + DT * CONV and not last:
                            conv((k + 2) // CHUNKS, (k + 2) % CHUNKS, k + 2, n - CONV_AT)
                        if n == PROJECT_AT and not (first and par == 0):
                            project(k - 1, final)
                    sum_states(k, STATES - 1)

            chunk_pairs(pe, body, nothing)
            project(BATCH * CHUNKS - 1, True)

        @block.vector
        def _(dve):
            dve.wait_ge(consts_in, 16 * 13)
            dve.wait_ge(setup_act, 2)
            dve.tensor_scalar(A_sb[:, :, :], A_sb[:, :, :], -1.0, None, ALU.mult).then_inc(setup_dve, 1)
            dve.tensor_tensor(tapT[:, :, :], wT[:, 0:INNER].rearrange("p (o d) -> p o d", o=1).broadcast_to([C, CONV, INNER]),
                              taps_row[:, :, :], ALU.mult).then_inc(setup_dve, 1)

            def take_remainder(k, par):
                dve.wait_ge(high_ready, k + 1)
                dve.wait_ge(parts_ready, k)
                dve.tensor_tensor(remainder[:, :], front_ps[0:DTR, 0, :], bc_parts[:, par, :],
                                  ALU.subtract).then_inc(remainder_ready, 1)

            def take_low(k, par):
                dve.wait_ge(middle_ready, k + 1)
                dve.tensor_tensor(bc_parts[2 * BC:DTR, par, :], remainder[2 * BC:DTR, :], middle[2 * BC:DTR, :],
                                  ALU.subtract).then_inc(low_ready, 1)

            def softplus_max(k):
                for dt in range(DT):
                    dve.wait_ge(dt_ps, k * DT + dt + 1)
                    dve.wait_ge(abs_ready, k * DT + dt + 1)
                    dve.wait_ge(delta_ready, k * DT)
                    dve.tensor_scalar(sp_max[:, dt, :], front_ps[:, 1 - dt, :], db[:, dt:dt + 1], 0.0, ALU.add,
                                      ALU.max).then_inc(max_ready, 1)

            def make_du(k, par):
                for dt in range(DT):
                    dve.wait_ge(delta_ready, k * DT + dt + 1)
                    dve.wait_ge(conv_ready, k * DT + dt + 1)
                    dve.tensor_tensor(du[:, par, dt, :], delta[:, par, dt, :], conv_out[:, par, dt, :],
                                      ALU.mult).then_inc(du_ready, 1)

            def add_skip(k, par):
                for dt in range(DT):
                    dve.wait_ge(summed, (k + 1) * STATES * DT + 4 - (DT - 1 - dt))
                    dve.wait_ge(out_ps, k)
                    dve.scalar_tensor_tensor(skip[:, dt, :], conv_out[:, par, dt, :], Dv[:, dt:dt + 1], y_ps[:, dt, :],
                                             ALU.mult, ALU.add).then_inc(skip_ready, 1)

            def finish(k):
                dve.wait_ge(out_ps, k + 1)
                dve.wait_ge(stored, k * 16)
                dve.scalar_tensor_tensor(outbuf[:, :], front_ps[:, 1, :], nb[:, :],
                                         x_sb[:, bass.ds(((k // CHUNKS) % 2) * XLEN + (k % CHUNKS) * T + HALO, T)], ALU.add,
                                         ALU.add).then_inc(out_ready, 1)

            def front_step(k, par, n):
                if n == HIGH_AT:
                    take_remainder(k, par)
                if n == MIDDLE_AT:
                    take_low(k, par)
                if n == SOFTPLUS_AT:
                    softplus_max(k)
                if n == DU_AT:
                    make_du(k, par)

            for n in range(STATES):
                front_step(0, 0, n)

            def start(b, more):
                dve.wait_ge(carried, b * (CHUNKS + 1))
                dve.memset(carry[:, :, :], 0.0).then_inc(carried, 1)

            def body(b, c, first, last):
                for par in range(2):
                    k = b * CHUNKS + c + par
                    final = last and par == 1
                    for n in range(STATES):
                        s = k * STATES + n
                        if n == 0:
                            dve.wait_ge(carried, b * (CHUNKS + 1) + c + par + 1)
                        dve.wait_ge(rows_filled, s + 1)
                        for dt in range(DT):
                            dve.wait_ge(scanned, s * DT + dt + 1)
                            dve.wait_ge(du_ready, k * DT + dt + 1)
                            dve.tensor_tensor(drive[:, n % 2, dt, :], du[:, par, dt, :], b_ps[:, n % 2, :],
                                              ALU.mult).then_inc(drive_ready, 1)
                        for dt in range(DT):
                            dve.wait_ge(decay_ready, s * DT + dt + 1)
                            dve.wait_ge(drive_ready, s * DT + dt + 5)
                            dve.tensor_tensor_scan(out=states[:, dt, n, :], data0=decay[:, n % 2, dt, :],
                                                   data1=drive[:, n % 2, dt, :], initial=carry[:, dt, n:n + 1],
                                                   op0=ALU.mult, op1=ALU.add).then_inc(scanned, 1)
                        if not final:
                            front_step(k + 1, 1 - par, n)
                        if not (first and par == 0):
                            if n == SKIP_AT:
                                add_skip(k - 1, 1 - par)
                            if n == FINISH_AT:
                                finish(k - 1)
                    dve.wait_ge(scanned, (k + 1) * (STATES * DT) + 4)
                    dve.tensor_copy(carry[:, :, :], states[:, :, :, T - 1]).then_inc(carried, 1)

            chunk_pairs(dve, body, start)
            add_skip(BATCH * CHUNKS - 1, 1)
            finish(BATCH * CHUNKS - 1)


def filtered_relu_phase(nc, x_in, up_filter, down_filter, gain, slope, clamp, up_places, down_places, out):
    f32 = mybir.dt.float32
    ALU, ACT, AX = mybir.AluOpType, mybir.ActivationFunctionType, mybir.AxisListType
    IMAGES, SIDE, _ = x_in.shape
    TAPS = up_filter.shape[1]
    BIG = up_places.shape[1]
    HALF = BIG // 2
    PAIRS = 16
    GROUP = 8
    ROUNDS = IMAGES // (2 * PAIRS)

    with ExitStack() as ctx:
        def sb(name, shape, dt=f32):
            return ctx.enter_context(nc.sbuf_tensor("fr_" + name, shape, dt))

        def ps(name, shape):
            return ctx.enter_context(nc.psum_tensor("fr_" + name, shape, f32))

        def sem(name):
            return ctx.enter_context(nc.semaphore("fr_" + name))

        x_sb = sb("x", [128, 2, GROUP, SIDE])
        up_twice = sb("up_twice", [128, BIG])
        up_blocks = sb("up_blocks", [128, 2, BIG])
        downT = sb("downT", [128, 2, SIDE])
        up_sel, down_sel = sb("up_sel", [128, BIG, TAPS]), sb("down_sel", [HALF, 2 * SIDE, TAPS])
        fu, fd = sb("fu", [128, TAPS]), sb("fd", [HALF, TAPS])
        gain_sb, slope_sb, clamp_sb = sb("gain", [128, 1]), sb("slope", [128, 1]), sb("clamp", [128, 1])
        consts = sb("consts", [128, 6])
        rows_up = sb("rows_up", [128, 2, BIG])
        negative = sb("negative", [HALF, 2, 2, 2 * BIG])
        leaky = sb("leaky", [HALF, 2, 2, 2 * BIG])
        clipped = sb("clipped", [128, 2, 2, 2 * BIG])
        rows_down = sb("rows_down", [128, 2, 2, 2 * SIDE])
        outbuf = sb("outbuf", [128, 2, GROUP, SIDE])

        up_ps = ps("up", [128, 2, 512])
        big_ps = ps("big", [128, 2, 2, 512])
        down_ps = ps("down", [128, 512])
        out_ps = ps("out", [128, 512])

        consts_in, setup, matrices = sem("consts_in"), sem("setup"), sem("matrices")
        x_loaded = [sem("x_loaded_even"), sem("x_loaded_odd")]
        up_done, rows_up_ready, big_done = sem("up_done"), sem("rows_up_ready"), sem("big_done")
        negative_ready, leaky_ready, clipped_ready = sem("negative_ready"), sem("leaky_ready"), sem("clipped_ready")
        down_done, rows_down_ready = sem("down_done"), sem("rows_down_ready")
        out_done, out_ready = sem("out_done"), sem("out_ready")
        stored = [sem("stored_even"), sem("stored_odd")]
        block = ctx.enter_context(nc.Block())

        def rounds(engine, body):
            body(0, True, False)
            with engine.Fori(1, ROUNDS - 1) as r:
                body(r, False, False)
            body(ROUNDS - 1, False, True)

        @block.sync
        def _(sp):
            column = lambda a: a.broadcast_to([128, 1])
            for dst, src in [(up_sel[:, :, :], up_places), (down_sel[:, :, :], down_places),
                             (fu[:, :], up_filter.broadcast_to([128, TAPS])),
                             (fd[:, :], down_filter.broadcast_to([HALF, TAPS])),
                             (gain_sb[:, :], column(gain)), (slope_sb[:, :], column(slope)),
                             (clamp_sb[:, :], column(clamp))]:
                sp.dma_start(dst, src).then_inc(consts_in, 16)

            def load(r, g):
                for half in range(2):
                    start = r * (2 * PAIRS) + g * (2 * GROUP) + half * GROUP
                    sp.dma_start(x_sb[half * SIDE:(half + 1) * SIDE, g, :, :],
                                 x_in[bass.ds(start, GROUP), :, :].rearrange("c h w -> h c w")).then_inc(x_loaded[g], 16)

            load(0, 0)
            load(0, 1)

            def body(r, first, last):
                for g in range(2):
                    if not last:
                        sp.wait_ge(up_done, r * PAIRS + (g + 1) * GROUP)
                        load(r + 1, g)
                    sp.wait_ge(out_ready, r * 2 + g + 1)
                    start = r * (2 * PAIRS) + g * (2 * GROUP)
                    sp.dma_start(out[bass.ds(start, 2 * GROUP), :, :].rearrange("(k c) h w -> (c h) k w", c=2),
                                 outbuf[:, g, :, :]).then_inc(stored[g], 16)

            rounds(sp, body)
            for s in stored:
                sp.wait_ge(s, 16 * ROUNDS)

        @block.scalar
        def _(act):
            act.wait_ge(matrices, 3)

            def take_rows(r, q):
                act.wait_ge(up_done, r * PAIRS + q + 1)
                act.activation(rows_up[:, q % 2, :], up_ps[:, q % 2, 0:BIG], ACT.Copy).then_inc(rows_up_ready, 1)

            def negatives(r, q):
                act.wait_ge(big_done, r * PAIRS + q + 1)
                act.activation(negative[:, q % 2, :, :], big_ps[0:HALF, q % 2, :, 0:2 * BIG], ACT.Relu,
                               scale=-1.0).then_inc(negative_ready, 1)

            def take_out(r, g):
                act.wait_ge(out_done, r * PAIRS + (g + 1) * GROUP)
                act.wait_ge(stored[g], r * 16)
                act.activation(outbuf[:, g, :, :], out_ps[:, :].rearrange("p (k w) -> p k w", k=GROUP), ACT.Copy,
                               scale=gain_sb[:, :]).then_inc(out_ready, 1)

            take_rows(0, 0)
            take_rows(0, 1)
            negatives(0, 0)

            def body(r, first, last):
                for q in range(PAIRS):
                    if not (last and q + 2 >= PAIRS):
                        take_rows(r, q + 2) if q + 2 < PAIRS else take_rows(r + 1, q + 2 - PAIRS)
                    if not (last and q + 1 >= PAIRS):
                        negatives(r, q + 1) if q + 1 < PAIRS else negatives(r + 1, 0)
                    if q == 0 and not first:
                        take_out(r - 1, 1)
                    if q == GROUP:
                        take_out(r, 0)

            rounds(act, body)
            take_out(ROUNDS - 1, 1)

        @block.tensor
        def _(pe):
            pe.wait_ge(matrices, 3)

            def up_rows(r, q):
                g, k = divmod(q, GROUP)
                if k == 0:
                    pe.wait_ge(x_loaded[g], (r + 1) * 32)
                if not (isinstance(r, int) and r == 0 and q < 2):
                    pe.wait_ge(rows_up_ready, r * PAIRS + q - 1)
                c = 2 * (k % 4)
                pe.matmul(up_ps[:, q % 2, 0:BIG], x_sb[:, g, c:c + 2, :].rearrange("h c w -> h (c w)"),
                          up_blocks[:, k // 4, :], start=True, stop=True).then_inc(up_done, 1)

            def up_columns(r, q):
                pe.wait_ge(rows_up_ready, r * PAIRS + q + 1)
                if not (isinstance(r, int) and r == 0 and q < 2):
                    pe.wait_ge(leaky_ready, r * PAIRS + q - 1)
                for tile in range(2):
                    last = pe.matmul(big_ps[0:HALF, q % 2, tile, 0:2 * BIG], rows_up[:, q % 2, tile * HALF:(tile + 1) * HALF],
                                     up_blocks[:, :, :].rearrange("p c w -> p (c w)"), start=True, stop=True)
                last.then_inc(big_done, 1)

            def down_rows(r, q):
                pe.wait_ge(clipped_ready, r * PAIRS + q + 1)
                pe.wait_ge(rows_down_ready, r * PAIRS + q)
                for tile in range(2):
                    for c in range(2):
                        for k in range(2):
                            c0 = c * BIG + tile * HALF
                            col = (tile * 2 + c) * SIDE
                            last = pe.matmul(down_ps[0:HALF, col:col + SIDE], clipped[:, q % 2, k, c0:c0 + HALF],
                                             downT[:, k, :], start=k == 0, stop=k == 1)
                last.then_inc(down_done, 1)

            def down_columns(r, q):
                pe.wait_ge(rows_down_ready, r * PAIRS + q + 1)
                if q % GROUP == 0:
                    pe.wait_ge(out_ready, r * 2 + q // GROUP)
                for k in range(2):
                    last = pe.matmul(out_ps[:, (q % GROUP) * SIDE:(q % GROUP + 1) * SIDE],
                                     rows_down[:, q % 2, k, :], downT[:, k, :], start=k == 0, stop=k == 1)
                last.then_inc(out_done, 1)

            up_rows(0, 0)
            up_rows(0, 1)
            up_columns(0, 0)

            def body(r, first, last):
                for q in range(PAIRS):
                    if not (last and q + 2 >= PAIRS):
                        up_rows(r, q + 2) if q + 2 < PAIRS else up_rows(r + 1, q + 2 - PAIRS)
                    if not (last and q + 1 >= PAIRS):
                        up_columns(r, q + 1) if q + 1 < PAIRS else up_columns(r + 1, 0)
                    down_rows(r, q)
                    if not (first and q == 0):
                        down_columns(r, q - 1) if q else down_columns(r - 1, PAIRS - 1)

            rounds(pe, body)
            down_columns(ROUNDS - 1, PAIRS - 1)

        @block.vector
        def _(dve):
            dve.wait_ge(consts_in, 16 * 7)
            step = [0]

            def done(instruction):
                step[0] += 1
                instruction.then_inc(setup, 1)
                dve.wait_ge(setup, step[0])

            done(dve.tensor_tensor(up_sel[:, :, :], up_sel[:, :, :],
                                   fu[:, :].rearrange("p (o k) -> p o k", o=1).broadcast_to([128, BIG, TAPS]), ALU.mult))
            done(dve.tensor_reduce(up_twice[:, :], up_sel[:, :, :], AX.X, ALU.add))
            done(dve.memset(up_blocks[:, :, :], 0.0))
            for c in range(2):
                rows = slice(c * SIDE, (c + 1) * SIDE)
                dve.tensor_scalar(up_blocks[rows, c, :], up_twice[rows, :], 2.0, None, ALU.mult).then_inc(matrices, 1)
            done(dve.memset(downT[:, :, :], 0.0))
            done(dve.memset(clipped[:, :, :, :], 0.0))
            done(dve.memset(rows_down[:, :, :, :], 0.0))
            done(dve.tensor_tensor(down_sel[:, :, :], down_sel[:, :, :],
                                   fd[:, :].rearrange("p (o k) -> p o k", o=1).broadcast_to([HALF, 2 * SIDE, TAPS]),
                                   ALU.mult))
            done(dve.tensor_scalar(consts[:, 0:1], slope_sb[:, :], -1.0, 1.0, ALU.mult, ALU.add))
            done(dve.tensor_scalar(consts[:, 1:2], gain_sb[:, :], -1.0, None, ALU.mult))
            done(dve.tensor_tensor(consts[:, 2:3], consts[:, 1:2], gain_sb[:, :], ALU.max))
            done(dve.reciprocal(consts[:, 3:4], consts[:, 2:3]))
            done(dve.tensor_tensor(consts[:, 4:5], consts[:, 3:4], clamp_sb[:, :], ALU.mult))
            done(dve.tensor_scalar(consts[:, 5:6], consts[:, 4:5], -1.0, None, ALU.mult))
            dve.tensor_reduce(downT[0:HALF, :, :].rearrange("p a b -> p (a b)"), down_sel[:, :, :], AX.X,
                              ALU.add).then_inc(matrices, 1)

            def activate(r, q):
                n = r * PAIRS + q
                dve.wait_ge(negative_ready, n + 1)
                if not (isinstance(r, int) and r == 0 and q < 2):
                    dve.wait_ge(clipped_ready, n - 1)
                dve.scalar_tensor_tensor(leaky[:, q % 2, :, :], negative[:, q % 2, :, :], consts[0:HALF, 0:1],
                                         big_ps[0:HALF, q % 2, :, 0:2 * BIG], ALU.mult, ALU.add).then_inc(leaky_ready, 1)
                dve.wait_ge(leaky_ready, n + 1)
                if not (isinstance(r, int) and r == 0 and q < 2):
                    dve.wait_ge(down_done, n - 1)
                dve.tensor_scalar(clipped[0:HALF, q % 2, :, :], leaky[:, q % 2, :, :], consts[0:HALF, 4:5],
                                  consts[0:HALF, 5:6], ALU.min, ALU.max).then_inc(clipped_ready, 1)

            def take_down(r, q):
                dve.wait_ge(down_done, r * PAIRS + q + 1)
                dve.tensor_copy(rows_down[0:HALF, q % 2, :, :].rearrange("p a b -> p (a b)"),
                                down_ps[0:HALF, 0:4 * SIDE]).then_inc(rows_down_ready, 1)

            activate(0, 0)

            def body(r, first, last):
                for q in range(PAIRS):
                    if not (last and q + 1 >= PAIRS):
                        activate(r, q + 1) if q + 1 < PAIRS else activate(r + 1, 0)
                    take_down(r, q)

            rounds(dve, body)


def dynamic_conv_phase(nc, x_in, w_fc1T, ln1_w, ln1_b, w_fc2T, ln2_w, ln2_b, w_expandT, w_shrinkT,
                       grn_gamma, grn_beta, centering, ident, out):
    f32 = mybir.dt.float32
    ALU, ACT, AX = mybir.AluOpType, mybir.ActivationFunctionType, mybir.AxisListType
    BATCH, C, L = x_in.shape
    SIDE = 64
    K = 5
    PAD = K // 2
    WIDE = SIDE + 2 * PAD
    CR = w_fc1T.shape[1]
    CE = w_expandT.shape[1]
    MT = CE // 128
    ROWS = 16
    N = ROWS * SIDE
    TILES = L // N
    PE_TAPS = 6
    TAPS = [(k // K, k % K) for k in range(K * K)]
    DVE_TAPS = K * K - PE_TAPS
    OUTS = L // 512
    EPS = 1e-6
    AT_LAST = 8
    BEFORE_GRN = 3
    UNITS = 2 * MT

    with ExitStack() as ctx:
        def sb(name, shape, dt=f32):
            return ctx.enter_context(nc.sbuf_tensor("dc_" + name, shape, dt))

        def ps(name, shape):
            return ctx.enter_context(nc.psum_tensor("dc_" + name, shape, f32))

        def sem(name):
            return ctx.enter_context(nc.semaphore("dc_" + name))

        xpad = sb("xpad", [C, 2, WIDE, WIDE])
        gelu = sb("gelu", [C, MT, L])
        acc = sb("acc", [C, 2, N])
        centred, squared = sb("centred", [C, N]), sb("squared", [C, N])
        normed = sb("normed", [C, N])
        square_scratch = sb("square_scratch", [C, N])
        outbuf = sb("outbuf", [C, 2, 512])
        diag = sb("diag", [C, PE_TAPS, C])
        fc1T, fc2T = sb("fc1T", [C, CR]), sb("fc2T", [CR, C * K * K])
        expT, expTs = sb("expT", [C, CE]), sb("expTs", [C, CE])
        shrT, shrTs = sb("shrT", [C, MT, C]), sb("shrTs", [C, MT, C])
        centre_sb, ident_sb = sb("centre", [C, C]), sb("ident", [C, C])
        l1w, l1b = sb("l1w", [1, CR]), sb("l1b", [1, CR])
        l2w, l2b = sb("l2w", [C, 1]), sb("l2b", [C, 1])
        gamma, beta = sb("gamma", [C, MT]), sb("beta", [C, MT])
        mean_col, mean_all = sb("mean_col", [C, 1]), sb("mean_all", [C, C])
        one, eps = sb("one", [1, 1]), sb("eps", [C, 1])
        gelu_bias, out_bias = sb("gelu_bias", [C, MT]), sb("out_bias", [C, 1])
        pooled = sb("pooled", [C, 1])
        hid = sb("hid", [1, 6, 64])
        hst = sb("hst", [1, 6])
        hidT = sb("hidT", [CR, 1])
        dyn = sb("dyn", [C, 2, K * K])
        dyn_pe = sb("dyn_pe", [C, PE_TAPS])
        std, rstd = sb("std", [128, N // 128]), sb("rstd", [128, N // 128])
        sums = sb("sums", [C, MT, TILES])
        sumsq, gx = sb("sumsq", [C, MT]), sb("gx", [C, MT])
        gm, ginv, nx, factor = sb("gm", [C, 1]), sb("ginv", [C, 2]), sb("nx", [C, MT]), sb("factor", [C, MT])

        conv_ps = ps("conv", [128, 2, 512])
        norm_ps = ps("norm", [128, 2, 512])
        exp_ps = ps("expand", [128, 2, 512])
        var_ps = ps("var", [128, 512])
        prep_ps = ps("prep", [128, 512])

        consts_in, made, setup_ps, setup = sem("consts_in"), sem("made"), sem("setup_ps"), sem("setup")
        x_loaded = sem("x_loaded")
        prep_pe, prep_dve, prep_act = sem("prep_pe"), sem("prep_dve"), sem("prep_act")
        diag_ready, hid_step = sem("diag_ready"), sem("hid_step")
        conv_ready, tap_done = sem("conv_ready"), sem("tap_done")
        centred_ps, centred_ready, squared_ready = sem("centred_ps"), sem("centred_ready"), sem("squared_ready")
        var_ready, std_ready, rstd_ready = sem("var_ready"), sem("std_ready"), sem("rstd_ready")
        rstd_ps, normed_ready = sem("rstd_ps"), sem("normed_ready")
        expanded, gelu_done, sum_done = sem("expanded"), sem("gelu_done"), sem("sum_done")
        grn_dve, gx_ready, gm_ps = sem("grn_dve"), sem("gx_ready"), sem("gm_ps")
        shrunk, out_ready = sem("shrunk"), sem("out_ready")
        stored = [sem("stored_even"), sem("stored_odd")]
        block = ctx.enter_context(nc.Block())

        PREP_DVE, GRN_DVE = 12, 10

        def batches(engine, body):
            body(0, False)
            with engine.Fori(1, BATCH - 1) as b:
                body(b, False)
            body(BATCH - 1, True)

        @block.sync
        def _(sp):
            for dst, src in [
                    (fc1T[:, :], w_fc1T), (fc2T[:, :], w_fc2T), (expT[:, :], w_expandT),
                    (shrT[:, :, :], w_shrinkT.rearrange("(m p) c -> p m c", p=128)),
                    (centre_sb[:, :], centering), (ident_sb[:, :], ident),
                    (l1w[:, :], ln1_w), (l1b[:, :], ln1_b), (l2w[:, :], ln2_w), (l2b[:, :], ln2_b),
                    (gamma[:, :], grn_gamma), (beta[:, :], grn_beta)]:
                sp.dma_start(dst, src).then_inc(consts_in, 16)
            sp.wait_ge(made, 1)
            image = x_in.rearrange("b c (h w) -> b c h w", h=SIDE)

            def load(b):
                sp.dma_start(xpad[:, bass.ds(b % 2, 1), PAD:PAD + SIDE, PAD:PAD + SIDE].rearrange("c o h w -> c (o h) w"),
                             image[bass.ds(b, 1), :, :, :].rearrange("o c h w -> (o c) h w")).then_inc(x_loaded, 16)

            load(0)
            sp.wait_ge(x_loaded, 16)

            def batch(b, last):
                if not last:
                    sp.wait_ge(out_ready, b * OUTS)
                    load(b + 1)
                for j in range(OUTS):
                    sp.wait_ge(out_ready, b * OUTS + j + 1)
                    sp.dma_start(out[bass.ds(b, 1), :, j * 512:(j + 1) * 512].rearrange("o c l -> (o c) l"),
                                 outbuf[:, j % 2, :]).then_inc(stored[j % 2], 16)

            batches(sp, batch)
            for s in stored:
                sp.wait_ge(s, 16 * BATCH * OUTS // 2)

        @block.gpsimd
        def _(pool):
            pool.memset(xpad[:, :, :, :], 0.0).then_inc(made, 1)
            pool.memset(mean_col[:, :], 1.0 / C).then_inc(made, 1)
            pool.memset(mean_all[:, :], 1.0 / CE).then_inc(made, 1)
            pool.memset(one[:, :], 1.0).then_inc(made, 1)
            pool.memset(eps[:, :], EPS).then_inc(made, 1)
            pool.memset(hid[:, :, :], 0.0).then_inc(made, 1)

        @block.scalar
        def _(act):
            act.wait_ge(consts_in, 16 * 12)
            act.wait_ge(made, 6)
            act.wait_ge(setup_ps, 1)
            act.activation(gelu_bias[:, :], prep_ps[:, 0:MT], ACT.Copy).then_inc(setup, 1)
            act.activation(out_bias[:, :], prep_ps[:, MT:MT + 1], ACT.Copy).then_inc(setup, 1)
            act.activation(expTs[:, :], expT[:, :], ACT.Copy, scale=l2w[:, :]).then_inc(setup, 1)

            def prepare_std(b):
                act.wait_ge(prep_dve, b * PREP_DVE + 5)
                act.activation(hst[:, 3:4], hst[:, 2:3], ACT.Sqrt, bias=eps[0:1, :],
                               scale=1.0 / CR).then_inc(prep_act, 1)

            def prepare_diag(b):
                act.wait_ge(prep_dve, b * PREP_DVE + PREP_DVE)
                act.wait_ge(conv_ready, b * TILES)
                for k in range(PE_TAPS):
                    last = act.activation(diag[:, k, :], ident_sb[:, :], ACT.Copy, scale=dyn_pe[:, k:k + 1])
                last.then_inc(diag_ready, 1)

            prepare_std(0)
            prepare_diag(0)

            def batch(b, last):
                for i in range(TILES):
                    t = b * TILES + i
                    act.wait_ge(centred_ps, t + 1)
                    act.wait_ge(normed_ready, t)
                    act.activation(centred[:, :], norm_ps[:, :, :].rearrange("p a c -> p (a c)"),
                                   ACT.Copy).then_inc(centred_ready, 1)
                    act.wait_ge(var_ready, t)
                    act.activation(squared[:, :], norm_ps[:, :, :].rearrange("p a c -> p (a c)"),
                                   ACT.Square).then_inc(squared_ready, 1)
                    act.wait_ge(var_ready, t + 1)
                    act.wait_ge(rstd_ready, t)
                    act.activation(std[:, :], var_ps[:, 0:N // 128], ACT.Sqrt, bias=eps[:, :]).then_inc(std_ready, 1)
                    for half in range(2):
                        if half and i == 0 and not last:
                            prepare_std(b + 1)
                        for m in range(MT):
                            u = half * MT + m
                            act.wait_ge(expanded, t * UNITS + u + 1)
                            c0 = i * N + half * 512
                            act.activation(gelu[:, m, c0:c0 + 512], exp_ps[:, u % 2, :], ACT.Gelu,
                                           bias=gelu_bias[:, m:m + 1]).then_inc(gelu_done, 1)
                    if i == 0 and not last:
                        prepare_diag(b + 1)
                    act.wait_ge(gelu_done, (t + 1) * UNITS)
                    for m in range(MT):
                        if i or m:
                            act.wait_ge(sum_done, (t * MT + m))
                        act.activation(square_scratch[:, :], gelu[:, m, i * N:(i + 1) * N], ACT.Square,
                                       accum_out=sums[:, m, i:i + 1]).then_inc(sum_done, 1)
                act.wait_ge(grn_dve, b * GRN_DVE + 1)
                act.activation(gx[:, :], sumsq[:, :], ACT.Sqrt).then_inc(gx_ready, 1)

            batches(act, batch)

        @block.tensor
        def _(pe):
            pe.wait_ge(consts_in, 16 * 12)
            pe.wait_ge(made, 6)
            for m in range(MT):
                pe.matmul(prep_ps[:, m:m + 1], expT[:, m * 128:(m + 1) * 128], l2b[:, :], start=True, stop=True)
            for m in range(MT):
                last = pe.matmul(prep_ps[:, MT:MT + 1], shrT[:, m, :], beta[:, m:m + 1], start=m == 0, stop=m == MT - 1)
            last.then_inc(setup_ps, 1)
            pe.wait_ge(setup, 3)

            def prepare(b):
                pe.wait_ge(prep_dve, b * PREP_DVE + 1)
                pe.matmul(prep_ps[0:1, 0:CR], pooled[:, :], fc1T[:, :], start=True, stop=True).then_inc(prep_pe, 1)
                pe.wait_ge(prep_dve, b * PREP_DVE + 9)
                pe.matmul(prep_ps[0:64, 64:65], hid[:, 5, :], one[:, :], start=True, stop=True).then_inc(prep_pe, 1)
                pe.wait_ge(prep_dve, b * PREP_DVE + 10)
                for k in range(K * K):
                    last = pe.matmul(prep_ps[:, 128 + k:129 + k], fc2T[:, k:C * K * K:K * K], hidT[:, :],
                                     start=True, stop=True)
                last.then_inc(prep_pe, 1)

            def conv(b, i):
                if i == 0:
                    pe.wait_ge(diag_ready, b + 1)
                    pe.wait_ge(x_loaded, 16 * (b + 1))
                t = b * TILES + i
                pe.wait_ge(tap_done, (t - 1) * DVE_TAPS + 1 if not (isinstance(t, int) and t == 0) else 0)
                for half in range(2):
                    for k in range(PE_TAPS):
                        dy, dx = TAPS[k]
                        r0 = i * ROWS + half * (ROWS // 2) + dy
                        last = pe.matmul(conv_ps[:, half, :], diag[:, k, :],
                                         xpad[:, bass.ds(b % 2, 1), r0:r0 + ROWS // 2, dx:dx + SIDE]
                                         .rearrange("c o h w -> c (o h) w"), start=k == 0, stop=k == PE_TAPS - 1)
                last.then_inc(conv_ready, 1)

            def norm_and_expand(b, i, last):
                t = b * TILES + i
                pe.wait_ge(tap_done, (t + 1) * DVE_TAPS)
                pe.wait_ge(normed_ready, t)
                for half in range(2):
                    last_mm = pe.matmul(norm_ps[:, half, :], centre_sb[:, :], acc[:, i % 2, half * 512:(half + 1) * 512],
                                     start=True, stop=True)
                last_mm.then_inc(centred_ps, 1)
                if i + 3 < TILES:
                    conv(b, i + 3)
                elif not last:
                    conv(b + 1, i + 3 - TILES)
                pe.wait_ge(squared_ready, t + 1)
                pe.wait_ge(std_ready, t)
                for j in range(N // 128):
                    last_mm = pe.matmul(var_ps[:, j:j + 1], squared[:, j * 128:(j + 1) * 128], mean_col[:, :],
                                     start=True, stop=True)
                last_mm.then_inc(var_ready, 1)
                pe.wait_ge(rstd_ready, t + 1)
                for j in range(N // 128):
                    last_mm = pe.matmul(norm_ps[:, j // 4, (j % 4) * 128:(j % 4 + 1) * 128],
                                     rstd[:, j:j + 1].broadcast_to([128, 128]), ident_sb[:, :], start=True, stop=True)
                last_mm.then_inc(rstd_ps, 1)
                pe.wait_ge(normed_ready, t + 1)
                if i == 0:
                    pe.wait_ge(out_ready, b * OUTS)
                for half in range(2):
                    if half and i == 0 and not last:
                        prepare(b + 1)
                    for m in range(MT):
                        u = half * MT + m
                        if i or u > 1:
                            pe.wait_ge(gelu_done, t * UNITS + u - 1)
                        pe.matmul(exp_ps[:, u % 2, :], expTs[:, m * 128:(m + 1) * 128],
                                  normed[:, half * 512:(half + 1) * 512], start=True, stop=True).then_inc(expanded, 1)

            prepare(0)
            conv(0, 0)
            conv(0, 1)
            conv(0, 2)

            def batch(b, last):
                for i in range(TILES):
                    norm_and_expand(b, i, last)
                pe.wait_ge(gx_ready, b + 1)
                pe.matmul(prep_ps[:, 256:256 + MT], mean_all[:, :], gx[:, :], start=True, stop=True).then_inc(gm_ps, 1)
                pe.wait_ge(grn_dve, (b + 1) * GRN_DVE)
                for j in range(OUTS):
                    pe.wait_ge(gelu_done, (b + 1) * TILES * UNITS)
                    if j >= 2:
                        pe.wait_ge(out_ready, b * OUTS + j - 1)
                    for m in range(MT):
                        last_mm = pe.matmul(exp_ps[:, j % 2, :], shrTs[:, m, :], gelu[:, m, j * 512:(j + 1) * 512],
                                            start=m == 0, stop=m == MT - 1)
                    last_mm.then_inc(shrunk, 1)

            batches(pe, batch)

        @block.vector
        def _(dve):
            dve.wait_ge(consts_in, 16 * 12)
            dve.wait_ge(made, 6)

            def prepare(b):
                step = [0]

                def done(instruction):
                    step[0] += 1
                    instruction.then_inc(prep_dve, 1)
                    dve.wait_ge(prep_dve, b * PREP_DVE + step[0])

                dve.wait_ge(x_loaded, 16 * (b + 1))
                done(dve.tensor_reduce(pooled[:, :], xpad[:, bass.ds(b % 2, 1), PAD:PAD + SIDE, PAD:PAD + SIDE]
                                       .rearrange("c o h w -> c (o h) w"), AX.XY, ALU.add))
                dve.wait_ge(prep_pe, 3 * b + 1)
                done(dve.tensor_scalar(hid[:, 0, 0:CR], prep_ps[0:1, 0:CR], 1.0 / L, None, ALU.mult))
                done(dve.tensor_reduce(hst[:, 0:1], hid[:, 0, 0:CR], AX.X, ALU.add))
                done(dve.tensor_scalar(hst[:, 1:2], hst[:, 0:1], -1.0 / CR, None, ALU.mult))
                dve.tensor_scalar(hid[:, 1, 0:CR], hid[:, 0, 0:CR], hst[:, 1:2], None, ALU.add).then_inc(hid_step, 1)
                dve.wait_ge(hid_step, 2 * b + 1)
                dve.tensor_tensor(hid[:, 2, 0:CR], hid[:, 1, 0:CR], hid[:, 1, 0:CR], ALU.mult).then_inc(hid_step, 1)
                dve.wait_ge(hid_step, 2 * b + 2)
                done(dve.tensor_reduce(hst[:, 2:3], hid[:, 2, 0:CR], AX.X, ALU.add))
                dve.wait_ge(prep_act, b + 1)
                done(dve.reciprocal(hst[:, 4:5], hst[:, 3:4]))
                done(dve.tensor_scalar(hid[:, 3, 0:CR], hid[:, 1, 0:CR], hst[:, 4:5], None, ALU.mult))
                done(dve.tensor_tensor(hid[:, 4, 0:CR], hid[:, 3, 0:CR], l1w[:, :], ALU.mult))
                done(dve.tensor_tensor(hid[:, 5, 0:CR], hid[:, 4, 0:CR], l1b[:, :], ALU.add))
                dve.wait_ge(prep_pe, 3 * b + 2)
                done(dve.tensor_copy(hidT[:, :], prep_ps[0:CR, 64:65]))

            def prepare_taps(b):
                dve.wait_ge(prep_pe, 3 * b + 3)
                dve.tensor_copy(dyn[:, bass.ds(b % 2, 1), :].rearrange("c o k -> c (o k)"),
                                prep_ps[:, 128:128 + K * K]).then_inc(prep_dve, 1)
                dve.wait_ge(prep_dve, b * PREP_DVE + PREP_DVE - 1)
                dve.wait_ge(diag_ready, b)
                dve.tensor_copy(dyn_pe[:, :], prep_ps[:, 128:128 + PE_TAPS]).then_inc(prep_dve, 1)
                dve.wait_ge(prep_dve, b * PREP_DVE + PREP_DVE)

            def taps(b, i, first, count):
                t = b * TILES + i
                for n in range(first, first + count):
                    dy, dx = TAPS[PE_TAPS + n]
                    view = xpad[:, bass.ds(b % 2, 1), i * ROWS + dy:i * ROWS + dy + ROWS, dx:dx + SIDE] \
                        .rearrange("c o h w -> c (o h) w")
                    mine = acc[:, i % 2, :].rearrange("c (h w) -> c h w", h=ROWS)
                    if n == 0:
                        dve.wait_ge(conv_ready, t + 1)
                        before = conv_ps[:, :, :].rearrange("c a (h w) -> c (a h) w", w=SIDE)
                    else:
                        dve.wait_ge(tap_done, t * DVE_TAPS + n)
                        before = mine
                    weight = dyn[:, bass.ds(b % 2, 1), PE_TAPS + n:PE_TAPS + n + 1].rearrange("c o k -> c (o k)")
                    dve.scalar_tensor_tensor(mine, view, weight, before, ALU.mult, ALU.add).then_inc(tap_done, 1)

            prepare(0)
            prepare_taps(0)
            taps(0, 0, 0, DVE_TAPS)
            taps(0, 1, 0, DVE_TAPS)

            def batch(b, last):
                for i in range(TILES):
                    t = b * TILES + i
                    nb, ni = (b, i + 2) if i + 2 < TILES else (b + 1, i + 2 - TILES)
                    has_next = not (last and i + 2 >= TILES)
                    if has_next:
                        dve.wait_ge(centred_ps, t + 1)
                        taps(nb, ni, 0, AT_LAST)
                    dve.wait_ge(std_ready, t + 1)
                    dve.wait_ge(rstd_ps, t)
                    dve.reciprocal(rstd[:, :], std[:, :]).then_inc(rstd_ready, 1)
                    if has_next and i + 1 < TILES:
                        taps(nb, ni, 8, 3)
                    dve.wait_ge(rstd_ps, t + 1)
                    dve.wait_ge(centred_ready, t + 1)
                    dve.wait_ge(expanded, t * UNITS)
                    dve.tensor_tensor(normed[:, :], norm_ps[:, :, :].rearrange("p a c -> p (a c)"), centred[:, :],
                                      ALU.mult).then_inc(normed_ready, 1)
                    if i == 0 and not last:
                        prepare(b + 1)
                    if has_next and i + 1 < TILES:
                        taps(nb, ni, 11, DVE_TAPS - 14)
                    if i == 0 and not last:
                        prepare_taps(b + 1)
                    if has_next and i + 1 < TILES:
                        taps(nb, ni, DVE_TAPS - 3, 3)
                step = [0]

                def done(instruction):
                    step[0] += 1
                    instruction.then_inc(grn_dve, 1)
                    dve.wait_ge(grn_dve, b * GRN_DVE + step[0])

                if not last:
                    taps(b + 1, 1, AT_LAST, BEFORE_GRN)
                dve.wait_ge(sum_done, (b + 1) * TILES * MT)
                done(dve.tensor_reduce(sumsq[:, :], sums[:, :, :], AX.X, ALU.add))
                dve.wait_ge(gm_ps, b + 1)
                done(dve.tensor_reduce(gm[:, :], prep_ps[:, 256:256 + MT], AX.X, ALU.add))
                done(dve.tensor_scalar(ginv[:, 0:1], gm[:, :], EPS, None, ALU.add))
                done(dve.reciprocal(ginv[:, 1:2], ginv[:, 0:1]))
                done(dve.scalar_tensor_tensor(nx[:, :], gx[:, :], ginv[:, 1:2], gamma[:, :], ALU.mult, ALU.mult))
                done(dve.tensor_scalar(factor[:, :], nx[:, :], 1.0, None, ALU.add))
                for m in range(MT):
                    done(dve.tensor_scalar(shrTs[:, m, :], shrT[:, m, :], factor[:, m:m + 1], None, ALU.mult))
                for j in range(OUTS):
                    dve.wait_ge(shrunk, b * OUTS + j + 1)
                    dve.wait_ge(stored[j % 2], (b * (OUTS // 2) + j // 2) * 16)
                    r0 = PAD + j * (512 // SIDE)
                    dve.scalar_tensor_tensor(
                        outbuf[:, j % 2, :].rearrange("c (h w) -> c h w", w=SIDE),
                        exp_ps[:, j % 2, :].rearrange("c (h w) -> c h w", w=SIDE), out_bias[:, :],
                        xpad[:, bass.ds(b % 2, 1), r0:r0 + 512 // SIDE, PAD:PAD + SIDE].rearrange("c o h w -> c (o h) w"),
                        ALU.add, ALU.add).then_inc(out_ready, 1)
                    if not last:
                        if j < DVE_TAPS - AT_LAST - BEFORE_GRN:
                            taps(b + 1, 1, AT_LAST + BEFORE_GRN + j, 1)

            batches(dve, batch)


def attention_phase(nc, x_in, gn_w, gn_b, w_qkv, w_qkvT, b_qkv, w_projT, b_proj,
                    rot_swapT, group_ones, ident, sin_table, cos_table, out):
    f32, f16 = mybir.dt.float32, mybir.dt.float16
    ALU, ACT, AX = mybir.AluOpType, mybir.ActivationFunctionType, mybir.AxisListType
    BATCH, C, L = x_in.shape
    HEADS = 4
    CH = C // HEADS
    TOKENS = 512
    CHUNKS = L // TOKENS
    KEY_TILES = L // 128
    PAIRS = KEY_TILES // 2
    QUERY_TILES = TOKENS // 128
    UNITS = QUERY_TILES * CHUNKS
    LEAD = 7
    SHIFT_ROW = 3 * CH
    KROWS = SHIFT_ROW + 1
    EPS = 1e-6
    GROUP_SIZE = C // 4 * L
    BLOCKS = CHUNKS * HEADS
    PROBS = 4
    VGROUPS = KEY_TILES // 4
    WINDOWS = L // 1024
    RESTACKS = 3 * HEADS
    N_LOADS = 15

    with ExitStack() as ctx:
        def sb(name, shape, dt=f32):
            return ctx.enter_context(nc.sbuf_tensor("at_" + name, shape, dt))

        def ps(name, shape):
            return ctx.enter_context(nc.psum_tensor("at_" + name, shape, f32))

        def sem(name):
            return ctx.enter_context(nc.semaphore("at_" + name))

        xn = sb("xn", [C, L])
        sin_sb, cos_sb = sb("sin", [C, L]), sb("cos", [C, L])
        qk_stack = sb("qk_stack", [KROWS, 2, HEADS, L], f16)
        q_stack, k_stack = qk_stack[:, 0, :, :], qk_stack[:, 1, :, :]
        v_stack = sb("v_stack", [128, KEY_TILES, HEADS, 3 * CH], f16)
        parts = sb("parts", [C, 4, 2, 1024], f16)
        cos_part = sb("cos_part", [C, 2, TOKENS])
        sin_part = sb("sin_part", [C, 2, TOKENS])
        rotated = sb("rotated", [C, 2, 2, TOKENS])
        v_rows = sb("v_rows", [128, 2, 4, C])
        probs = sb("probs", [128, PROBS, 2 * TOKENS], f16)
        unit_max = sb("unit_max", [128, 2, QUERY_TILES, CHUNKS])
        row_max = sb("row_max", [128, 2, QUERY_TILES])
        neg_max = sb("neg_max", [128, 2, QUERY_TILES], f16)
        out_hi, out_lo, den = sb("out_hi", [C, TOKENS]), sb("out_lo", [C, TOKENS]), sb("den", [C, TOKENS])
        inv_den = sb("inv_den", [C, TOKENS])
        out_sum = sb("out_sum", [C, TOKENS])
        attended = sb("attended", [C, TOKENS])
        result = sb("result", [C, TOKENS])
        wT = sb("wT", [C, 3 * C])
        w_rows = sb("w_rows", [C, 2, C])
        w_swapT = sb("w_swapT", [C, 2, C])
        projT = sb("projT", [C, C])
        swapT_sb = sb("swapT", [C, C])
        group_sb = sb("group", [C, C])
        ident32 = sb("ident32", [C, C])
        ident16 = sb("ident16", [C, C], f16)
        bqk = sb("bqk", [C, 2])
        bqk_swap = sb("bqk_swap", [C, 2])
        bv_row = sb("bv_row", [128, C])
        gw, gb, bp = sb("gw", [C, 1]), sb("gb", [C, 1]), sb("bp", [C, 1])
        x_sum, neg_mean = sb("x_sum", [C, 1]), sb("neg_mean", [C, 1])
        sq_parts, sq_sum = sb("sq_parts", [C, 2]), sb("sq_sum", [C, 1])
        var, std, inv_std = sb("var", [C, 1]), sb("std", [C, 1]), sb("inv_std", [C, 1])
        gain, offset = sb("gain", [C, 1]), sb("offset", [C, 1])

        shared = ps("shared", [128, 2, 512])
        s_ps = ps("scores", [128, 2, 2, 512])
        o_ps = ps("out", [128, 2, 512])

        consts_in = sem("consts_in")
        ones_made = sem("ones_made")
        swap_ps = sem("swap_ps")
        weights_ready = sem("weights_ready")
        x_loaded = sem("x_loaded")
        stat_step = sem("stat_step")
        mean_ps = sem("mean_ps")
        squares = sem("squares")
        var_ps = sem("var_ps")
        std_ready = sem("std_ready")
        xn_ready = sem("xn_ready")
        qk_ps = sem("qk_ps")
        rot_step = sem("rot_step")
        hi_ready = sem("hi_ready")
        lo_ready = sem("lo_ready")
        stacked = [sem("stacked_even"), sem("stacked_odd")]
        v_ps = sem("v_ps")
        v_sum = sem("v_sum")
        v_hi_ready = sem("v_hi_ready")
        v_lo_ready = sem("v_lo_ready")
        shared_filled = sem("shared_filled")
        shared_free = sem("shared_free")
        max_step = sem("max_step")
        scores_ready = sem("scores_ready")
        exps_done = sem("exps_done")
        probs_free = sem("probs_free")
        sum_ready, mean_ready = sem("sum_ready"), sem("mean_ready")
        sq_ready, var_ready = sem("sq_ready"), sem("var_ready")
        rot_ready = sem("rot_ready")
        out_free = sem("out_free")
        inv_ready = sem("inv_ready")
        sum_out = sem("sum_out")
        attended_ready = sem("attended_ready")
        stored = sem("stored")
        block = ctx.enter_context(nc.Block())

        def uses_of(h, first, last):
            uses = []
            for i in range(UNITS):
                blk, unit = divmod((h + 1) * UNITS + LEAD + i, UNITS)
                if last and blk >= HEADS:
                    continue
                uses.append((i // 2, "unit", blk, unit))
                if unit == UNITS - 1:
                    uses += [(i // 2 + 2, "row", blk, 0)]
            if h == 0 and not first:
                uses += [(9, "project", -1, 0), (9, "project", -1, 1)]
            return sorted(uses, key=lambda use: use[0])

        PROLOGUE = [(0, "unit", 0, i) for i in range(UNITS)] + [(0, "unit", 1, 0), (0, "unit", 1, 1)] \
            + [(0, "row", 0, 0)] + [(0, "unit", 1, i) for i in range(2, LEAD)]
        ROW_0 = 1 + PROLOGUE.index((0, "row", 0, 0))
        N_FIRST, N_MID, N_LAST = (sum(len(uses_of(h, f, l)) for h in range(HEADS))
                                  for f, l in ((True, False), (False, False), (False, True)))
        USES = len(PROLOGUE) + N_FIRST + N_MID * (CHUNKS - 2) + N_LAST + 2
        assert all(n % 2 == 0 for n in (len(PROLOGUE), N_FIRST, N_MID, N_LAST))

        PROJECTED = 1 + [use[1:] for use in uses_of(0, False, False)].index(("project", -1, 1))
        assert uses_of(0, False, True)[PROJECTED - 1][1:] == ("project", -1, 1)

        def row_position(h, first, last):
            at, found = 0, None
            for hh in range(HEADS):
                for use in uses_of(hh, first, last):
                    at += 1
                    if use[1:] == ("row", h, 0):
                        found = at
            return found

        def row_from_before(last_before):
            n = {False: N_MID}[last_before]
            at = 0
            for hh in range(HEADS):
                for use in uses_of(hh, False, False):
                    at += 1
                    if use[1:] == ("row", HEADS, 0):
                        return n - at

        def chunks_of(engine, body):
            body(0, True, False, len(PROLOGUE))
            with engine.Fori(1, CHUNKS - 1) as t:
                body(t, False, False, len(PROLOGUE) + N_FIRST - N_MID + t * N_MID)
            body(CHUNKS - 1, False, True, len(PROLOGUE) + N_FIRST + N_MID * (CHUNKS - 2))

        def batches(engine, batch):
            batch(0)
            with engine.Fori(1, BATCH) as b:
                batch(b)

        @block.sync
        def _(sp):
            loads = [(wT[:, :], w_qkvT), (w_rows[:, 0, :], w_qkv[0:C, :]), (w_rows[:, 1, :], w_qkv[C:2 * C, :]),
                     (swapT_sb[:, :], rot_swapT), (group_sb[:, :], group_ones), (ident32[:, :], ident),
                     (bqk[:, 0:1], b_qkv[0:C, :]), (bqk[:, 1:2], b_qkv[C:2 * C, :]),
                     (bv_row[:, :], b_qkv[2 * C:3 * C, :].rearrange("c o -> o c").broadcast_to([128, C])),
                     (gw[:, :], gn_w), (gb[:, :], gn_b), (bp[:, :], b_proj),
                     (sin_sb[:, :], sin_table), (cos_sb[:, :], cos_table), (projT[:, :], w_projT)]
            assert len(loads) == N_LOADS
            for dst, src in loads:
                sp.dma_start(dst, src).then_inc(consts_in, 16)
            def batch(b):
                sp.wait_ge(shared_free, b * USES + 2)
                sp.dma_start(xn[:, :], x_in[bass.ds(b, 1), :, :].rearrange("a c l -> (a c) l")).then_inc(x_loaded, 16)
                for w in range(WINDOWS):
                    sp.wait_ge(lo_ready, b * (2 * CHUNKS) + (w + 1) * 4)
                    for h in range(HEADS):
                        for row, q_part, k_part in ((0, 0, 2), (1, 0, 3), (2, 1, 2)):
                            sp.dma_start(qk_stack[CH * row:CH * row + CH, :, h, w * 1024:(w + 1) * 1024],
                                         parts[CH * h:CH * h + CH, q_part:k_part + 1:k_part - q_part, w % 2, :]
                                         ).then_inc(stacked[w % 2], 16)

                def store(t, uses):
                    sp.wait_ge(shared_free, b * USES + uses + 2)
                    sp.dma_start(out[bass.ds(b, 1), :, bass.ds(t * TOKENS, TOKENS)].rearrange("a c l -> (a c) l"),
                                 result[:, :]).then_inc(stored, 16)

                with sp.Fori(0, CHUNKS - 1) as t:
                    store(t, len(PROLOGUE) + N_FIRST + t * N_MID + PROJECTED)
                store(CHUNKS - 1, USES)

            batches(sp, batch)
            sp.wait_ge(stored, 16 * BATCH * CHUNKS + 1)

        @block.gpsimd
        def _(pool):
            pool.memset(k_stack[SHIFT_ROW:KROWS, :, :], 1.0).then_inc(ones_made, 1)
            pool.wait_ge(ones_made, 1)
            pool.memset(v_stack[:, :, :, 64:96], 1.0).then_inc(ones_made, 1)
            def batch(b):
                for c in range(CHUNKS):
                    for o in range(2):
                        cols = slice((c % 2) * TOKENS, (c % 2 + 1) * TOKENS)
                        pool.wait_ge(hi_ready, b * (2 * CHUNKS) + 2 * c + o + 1)
                        pool.tensor_tensor(parts[:, 2 * o + 1, (c // 2) % 2, cols], rotated[:, o, c % 2, :],
                                           parts[:, 2 * o, (c // 2) % 2, cols], ALU.subtract).then_inc(lo_ready, 1)
                for g in range(VGROUPS):
                    pool.wait_ge(v_hi_ready, b * VGROUPS + g + 1)
                    for t in range(4):
                        last = pool.tensor_tensor(v_stack[:, 4 * g + t, :, 32:64],
                                                  v_rows[:, g % 2, t, :].rearrange("p (h c) -> p h c", h=HEADS),
                                                  v_stack[:, 4 * g + t, :, 0:32], ALU.subtract)
                    last.then_inc(v_lo_ready, 1)
                with pool.Fori(0, CHUNKS) as t:
                    pool.wait_ge(out_free, (b * CHUNKS + t + 1) * HEADS + 2)
                    pool.tensor_tensor(out_sum[:, :], out_hi[:, :], out_lo[:, :], ALU.add).then_inc(sum_out, 1)
                    pool.wait_ge(sum_out, b * CHUNKS + t + 1)
                    pool.wait_ge(inv_ready, (b * CHUNKS + t + 1) * QUERY_TILES)
                    pool.tensor_tensor(attended[:, :], out_sum[:, :], inv_den[:, :], ALU.mult).then_inc(attended_ready, 1)

            batches(pool, batch)

        @block.scalar
        def _(act):
            act.wait_ge(consts_in, 16 * N_LOADS)
            act.activation(ident16[:, :], ident32[:, :], ACT.Copy).then_inc(weights_ready, 1)
            act.wait_ge(swap_ps, 1)
            act.activation(w_swapT[:, :, :].rearrange("p a c -> p (a c)"), s_ps[:, 0, 0, 0:2 * C],
                           ACT.Copy).then_inc(weights_ready, 1)
            act.activation(bqk_swap[:, :], s_ps[:, 0, 1, 0:2], ACT.Copy).then_inc(weights_ready, 1)
            def batch(b):
                act.wait_ge(mean_ready, b + 1)
                for half in range(2):
                    if half:
                        act.wait_ge(squares, 2 * b + 1)
                    act.activation(s_ps[:, :, :, :].rearrange("p a b c -> p (a b c)"),
                                   xn[:, half * 2048:(half + 1) * 2048], ACT.Square, bias=neg_mean[:, :],
                                   accum_out=sq_parts[:, half:half + 1]).then_inc(squares, 1)
                act.wait_ge(var_ready, b + 1)
                act.activation(std[:, :], var[:, :], ACT.Sqrt).then_inc(std_ready, 1)
                for c in range(CHUNKS):
                    for o in range(2):
                        cols = slice((c % 2) * TOKENS, (c % 2 + 1) * TOKENS)
                        act.wait_ge(rot_ready, b * (2 * CHUNKS) + 2 * c + o + 1)
                        if c % 2 == 0 and o == 0:
                            per = RESTACKS * 16
                            act.wait_ge(stacked[(c // 2) % 2], b * (WINDOWS // 2 * per) + (c // 4) * per)
                        act.activation(parts[:, 2 * o, (c // 2) % 2, cols], rotated[:, o, c % 2, :],
                                       ACT.Copy).then_inc(hi_ready, 1)
                for g in range(VGROUPS):
                    act.wait_ge(v_sum, b * VGROUPS + g + 1)
                    for t in range(4):
                        last = act.activation(v_stack[:, 4 * g + t, :, 0:32],
                                              v_rows[:, g % 2, t, :].rearrange("p (h c) -> p h c", h=HEADS), ACT.Copy)
                    last.then_inc(v_hi_ready, 1)

                def gather(h, n, pieces=(0, 1, 2)):
                    if 0 in pieces:
                        act.wait_ge(probs_free, (n + 1) * PAIRS + PROBS)
                    rows = slice(CH * h, CH * h + CH)
                    for i in pieces:
                        last = act.activation((out_hi, out_lo, den)[i][rows, :], o_ps[CH * i:CH * i + CH, h % 2, :],
                                              ACT.Copy)
                    if 2 in pieces:
                        last.then_inc(out_free, 1)

                def chunk(t, first, last, base):
                    for h in range(HEADS):
                        n = b * BLOCKS + t * HEADS + h
                        for u in range(PAIRS):
                            g = n * PAIRS + u
                            act.wait_ge(probs_free, g + 1)
                            act.wait_ge(scores_ready, g + 1)
                            act.activation(probs[:, u % PROBS, :], s_ps[:, u % 2, :, :].rearrange("p a c -> p (a c)"),
                                           ACT.Exp).then_inc(exps_done, 1)
                            if 2 <= u < 5 and not (first and h == 0):
                                if h == 1 and u == 2:
                                    act.wait_ge(attended_ready, b * CHUNKS + t + 1)
                                gather((h - 1) % HEADS, n - 1, (u - 2,))

                chunks_of(act, chunk)
                gather(HEADS - 1, (b + 1) * BLOCKS - 1)

            batches(act, batch)

        @block.tensor
        def _(pe):
            pe.sem_inc(shared_free, 2)
            pe.sem_inc(out_free, 2)
            pe.sem_inc(probs_free, PROBS)
            pe.sem_inc(attended_ready, 1)
            pe.sem_inc(stored, 1)
            pe.wait_ge(consts_in, 16 * N_LOADS)
            for o in range(2):
                pe.matmul(s_ps[:, 0, 0, o * C:(o + 1) * C], w_rows[:, o, :], swapT_sb[:, :], start=True, stop=True)
            pe.matmul(s_ps[:, 0, 1, 0:2], swapT_sb[:, :], bqk[:, :], start=True, stop=True).then_inc(swap_ps, 1)
            pe.wait_ge(weights_ready, 3)
            pe.wait_ge(ones_made, 2)

            def fill(use, t, position):
                _, kind, blk, part = use
                bank = position[1] % 2
                pe.wait_ge(shared_free, position[0] + 1)
                if kind == "unit":
                    q_tile, key_chunk = divmod(part, CHUNKS)
                    start = (t + blk // HEADS) * TOKENS + q_tile * 128
                    pe.matmul(shared[:, bank, :], q_stack[0:SHIFT_ROW, blk % HEADS, bass.ds(start, 128)],
                              k_stack[0:SHIFT_ROW, blk % HEADS, key_chunk * TOKENS:(key_chunk + 1) * TOKENS],
                              start=True, stop=True).then_inc(shared_filled, 1)
                elif kind == "row":
                    pe.wait_ge(max_step, position[2])
                    for j in range(QUERY_TILES):
                        last = pe.matmul(shared[SHIFT_ROW:KROWS, bank, j * 128:(j + 1) * 128],
                                         neg_max[:, blk % 2, j:j + 1], ident16[:, :],
                                         start=True, stop=True)
                    last.then_inc(shared_filled, 1)
                else:
                    pe.wait_ge(attended_ready, position[3] + 1)
                    last = pe.matmul(shared[:, bank, 0:256], projT[:, :], attended[:, part * 256:(part + 1) * 256],
                                     start=True, stop=True)
                    last.then_inc(shared_filled, 1)

            def batch(b):
                pe.wait_ge(sum_ready, b + 1)
                pe.matmul(o_ps[:, 0, 0:1], group_sb[:, :], x_sum[:, :], start=True, stop=True).then_inc(mean_ps, 1)
                pe.wait_ge(sq_ready, b + 1)
                pe.matmul(o_ps[:, 1, 0:1], group_sb[:, :], sq_sum[:, :], start=True, stop=True).then_inc(var_ps, 1)
                pe.wait_ge(xn_ready, b + 1)
                for c in range(CHUNKS):
                    for o in range(2):
                        if c:
                            pe.wait_ge(rot_ready, b * (2 * CHUNKS) + 2 * (c - 1) + o + 1)
                        pe.matmul(s_ps[:, o, 0, :], wT[:, o * C:(o + 1) * C], xn[:, c * TOKENS:(c + 1) * TOKENS],
                                  start=True, stop=True)
                        pe.matmul(s_ps[:, o, 1, :], w_swapT[:, o, :], xn[:, c * TOKENS:(c + 1) * TOKENS],
                                  start=True, stop=True).then_inc(qk_ps, 1)
                for g in range(VGROUPS):
                    if g >= 2:
                        pe.wait_ge(v_sum, b * VGROUPS + g - 1)
                    for t in range(4):
                        s0 = (4 * g + t) * 128
                        last = pe.matmul(o_ps[:, g % 2, t * C:(t + 1) * C], xn[:, s0:s0 + 128], wT[:, 2 * C:3 * C],
                                         start=True, stop=True)
                    last.then_inc(v_ps, 1)
                for s in stacked:
                    pe.wait_ge(s, (b + 1) * (WINDOWS // 2 * RESTACKS * 16))
                rows = b * BLOCKS
                for i, use in enumerate(PROLOGUE):
                    fill(use, 0, (b * USES + i, i, rows * 2 + 2, None))
                pe.wait_ge(v_lo_ready, (b + 1) * VGROUPS)

                def weighted_sum(h, u, t, n):
                    pe.wait_ge(exps_done, n * PAIRS + u + 1)
                    if u == 0:
                        pe.wait_ge(out_free, n + 1)
                    for j in range(2):
                        last = pe.matmul(o_ps[0:3 * CH, h % 2, :], v_stack[:, 2 * u + j, h, :],
                                         probs[:, u % PROBS, j * TOKENS:(j + 1) * TOKENS],
                                         start=u == 0 and j == 0, stop=u == PAIRS - 1 and j == 1)
                    last.then_inc(probs_free, 1)

                def scores(h, u, t, first, last, n0, base):
                    if u == 0:
                        if h == 0 and first:
                            done = b * USES + ROW_0
                        elif h == 0:
                            done = b * USES + base - row_from_before(False)
                        else:
                            done = b * USES + base + row_position(h, first, last)
                        pe.wait_ge(shared_free, done + 2)
                    if not (first and h == 0 and u < 2):
                        pe.wait_ge(exps_done, (n0 + h) * PAIRS + u - 1)
                    for j in range(2):
                        key = (2 * u + j) * 128
                        last_mm = pe.matmul(s_ps[:, u % 2, j, :], k_stack[:, h, key:key + 128],
                                            q_stack[:, h, bass.ds(t * TOKENS, TOKENS)], start=True, stop=True)
                    last_mm.then_inc(scores_ready, 1)

                def chunk(t, first, last, base):
                    at = 0
                    n0 = b * BLOCKS + t * HEADS
                    for h in range(HEADS):
                        uses = uses_of(h, first, last)
                        for u in range(PAIRS):
                            now = [x for x in uses if x[0] == u or (u == PAIRS - 1 and x[0] > u)]
                            for i, use in enumerate(now):
                                if i == len(now) // 2:
                                    scores(h, u, t, first, last, n0, base)
                                fill(use, t, (b * USES + base + at, at, (b * BLOCKS + t * HEADS + use[2]) * 2 + 2,
                                              b * CHUNKS + t))
                                at += 1
                            if not now:
                                scores(h, u, t, first, last, n0, base)
                            if not (first and h == 0 and u == 0):
                                if u:
                                    weighted_sum(h, u - 1, t, n0 + h)
                                else:
                                    weighted_sum((h - 1) % HEADS, PAIRS - 1, t, n0 + h - 1)

                chunks_of(pe, chunk)
                end = (b + 1) * BLOCKS
                weighted_sum(HEADS - 1, PAIRS - 1, None, end - 1)
                for half in range(2):
                    fill((0, "project", -1, half), None, (b * USES + USES - 2 + half, half, None, (b + 1) * CHUNKS))

            batches(pe, batch)

        @block.vector
        def _(dve):
            dve.wait_ge(consts_in, 16 * N_LOADS)
            dve.wait_ge(weights_ready, 3)

            def drain(use, t, position, n_row):
                _, kind, blk, part = use
                bank = position[1] % 2
                dve.wait_ge(shared_filled, position[0] + 1)
                if kind == "unit":
                    q_tile, key_chunk = divmod(part, CHUNKS)
                    dve.tensor_reduce(unit_max[:, blk % 2, q_tile, key_chunk:key_chunk + 1], shared[:, bank, :],
                                      AX.X, ALU.max).then_inc(shared_free, 1)
                    if part == UNITS - 1:
                        dve.wait_ge(shared_free, position[0] + 3)
                        dve.tensor_reduce(row_max[:, blk % 2, :], unit_max[:, blk % 2, :, :],
                                          AX.X, ALU.max).then_inc(max_step, 1)
                        dve.wait_ge(max_step, n_row * 2 + 1)
                        dve.tensor_scalar(neg_max[:, blk % 2, :], row_max[:, blk % 2, :], -1.0, None,
                                          ALU.mult).then_inc(max_step, 1)
                elif kind == "row":
                    col = (t + blk // HEADS) * TOKENS
                    dve.tensor_copy(q_stack[SHIFT_ROW:KROWS, blk % HEADS, bass.ds(col, TOKENS)],
                                    shared[SHIFT_ROW:KROWS, bank, :]).then_inc(shared_free, 1)
                else:
                    if part == 0:
                        dve.wait_ge(stored, n_row * 16 + 1)
                    col = t * TOKENS + part * 256
                    last = dve.scalar_tensor_tensor(result[:, part * 256:(part + 1) * 256], shared[:, bank, 0:256],
                                                    bp[:, :], xn[:, bass.ds(col, 256)], ALU.add, ALU.add)
                    last.then_inc(shared_free, 1)

            def invert(t, piece):
                if piece == 0:
                    dve.wait_ge(out_free, (t + 1) * HEADS + 2)
                    dve.wait_ge(attended_ready, t + 1)
                cols = slice(piece * 128, (piece + 1) * 128)
                dve.reciprocal(inv_den[:, cols], den[:, cols]).then_inc(inv_ready, 1)

            def batch(b):
                dve.wait_ge(x_loaded, (b + 1) * 16)
                dve.tensor_reduce(x_sum[:, :], xn[:, :], AX.X, ALU.add).then_inc(sum_ready, 1)
                dve.wait_ge(mean_ps, b + 1)
                dve.tensor_scalar(neg_mean[:, :], o_ps[:, 0, 0:1], -1.0 / GROUP_SIZE, None, ALU.mult).then_inc(mean_ready, 1)
                dve.wait_ge(squares, 2 * b + 2)
                dve.tensor_tensor(sq_sum[:, :], sq_parts[:, 0:1], sq_parts[:, 1:2], ALU.add).then_inc(sq_ready, 1)
                dve.wait_ge(var_ps, b + 1)
                dve.tensor_scalar(var[:, :], o_ps[:, 1, 0:1], 1.0 / (GROUP_SIZE - 1), EPS, ALU.mult,
                                  ALU.add).then_inc(var_ready, 1)
                dve.wait_ge(std_ready, b + 1)
                dve.reciprocal(inv_std[:, :], std[:, :]).then_inc(stat_step, 1)
                dve.wait_ge(stat_step, 3 * b + 1)
                dve.tensor_tensor(gain[:, :], inv_std[:, :], gw[:, :], ALU.mult).then_inc(stat_step, 1)
                dve.wait_ge(stat_step, 3 * b + 2)
                dve.scalar_tensor_tensor(offset[:, :], neg_mean[:, :], gain[:, :], gb[:, :], ALU.mult,
                                         ALU.add).then_inc(stat_step, 1)
                dve.wait_ge(stat_step, 3 * b + 3)
                dve.tensor_scalar(xn[:, :], xn[:, :], gain[:, :], offset[:, :], ALU.mult, ALU.add).then_inc(xn_ready, 1)
                for c in range(CHUNKS):
                    for o in range(2):
                        k = b * (2 * CHUNKS) + 2 * c + o
                        cols = slice(c * TOKENS, (c + 1) * TOKENS)
                        if c:
                            dve.wait_ge(rot_ready, k - 1)
                        dve.wait_ge(qk_ps, k + 1)
                        dve.scalar_tensor_tensor(cos_part[:, o, :], s_ps[:, o, 0, :], bqk[:, o:o + 1], cos_sb[:, cols],
                                                 ALU.add, ALU.mult).then_inc(rot_step, 1)
                        dve.scalar_tensor_tensor(sin_part[:, o, :], s_ps[:, o, 1, :], bqk_swap[:, o:o + 1],
                                                 sin_sb[:, cols], ALU.add, ALU.mult).then_inc(rot_step, 1)
                        dve.wait_ge(rot_step, 2 * k + 2)
                        if c >= 2:
                            dve.wait_ge(lo_ready, k - 3)
                        dve.tensor_tensor(rotated[:, o, c % 2, :], cos_part[:, o, :], sin_part[:, o, :],
                                          ALU.add).then_inc(rot_ready, 1)
                for g in range(VGROUPS):
                    dve.wait_ge(v_ps, b * VGROUPS + g + 1)
                    if g >= 2:
                        dve.wait_ge(v_lo_ready, b * VGROUPS + g - 1)
                    dve.tensor_tensor(v_rows[:, g % 2, :, :], o_ps[:, g % 2, :].rearrange("p (t c) -> p t c", t=4),
                                      bv_row[:, :].rearrange("p (o c) -> p o c", o=1).broadcast_to([128, 4, C]),
                                      ALU.add).then_inc(v_sum, 1)
                for i, use in enumerate(PROLOGUE):
                    drain(use, 0, (b * USES + i, i), b * BLOCKS)

                def chunk(t, first, last, base):
                    at = 0
                    n0 = b * BLOCKS + t * HEADS
                    for h in range(HEADS):
                        uses = uses_of(h, first, last)
                        for u in range(PAIRS):
                            for use in [x for x in uses if x[0] == u or (u == PAIRS - 1 and x[0] > u)]:
                                if use[1] == "project":
                                    drain(use, t - 1, (b * USES + base + at, at), b * CHUNKS + t - 1)
                                else:
                                    drain(use, t, (b * USES + base + at, at), n0 + use[2])
                                at += 1
                            if h == 0 and not first and 4 <= u < 4 + QUERY_TILES:
                                invert(b * CHUNKS + t - 1, u - 4)

                chunks_of(dve, chunk)
                for piece in range(QUERY_TILES):
                    invert(b * CHUNKS + CHUNKS - 1, piece)
                for half in range(2):
                    drain((0, "project", -1, half), CHUNKS - 1, (b * USES + USES - 2 + half, half),
                          b * CHUNKS + CHUNKS - 1)

            batches(dve, batch)


def build_program(nc, t, out):
    f32 = mybir.dt.float32
    batch, channels, tokens = t["x"].shape
    side = 64
    x0 = nc.dram_tensor("x0", [batch, channels, tokens], f32, kind="Internal").ap()
    x1 = nc.dram_tensor("x1", [batch, channels, tokens], f32, kind="Internal").ap()
    x2 = nc.dram_tensor("x2", [batch, channels, tokens], f32, kind="Internal").ap()

    def images(a):
        return a.rearrange("b c (h w) -> (b c) h w", h=side)

    mamba_phase(nc, t["x"], t["proj_w"], t["in_projT"], t["conv_wT"], t["conv_b"], t["x_proj_cols"],
                t["dt_projT"], t["dt_b"], t["A_log"], t["D"], t["out_projT"], t["next_bias"], t["ident"],
                t["row_select"], x0)
    filtered_relu_phase(nc, images(x0), t["up_filter"], t["down_filter"], t["gain"], t["slope"], t["clamp"],
                        t["up_places"], t["down_places"], images(x1))
    dynamic_conv_phase(nc, x1, t["w_fc1T"], t["ln1_w"], t["ln1_b"], t["w_fc2T"], t["ln2_w"], t["ln2_b"],
                       t["w_expandT"], t["w_shrinkT"], t["grn_gamma"], t["grn_beta"], t["centering"],
                       t["ident"], x2)
    attention_phase(nc, x2, t["gn_w"], t["gn_b"], t["w_qkv"], t["w_qkvT"], t["b_qkv"], t["w_projT"],
                    t["b_proj"], t["rot_swapT"], t["group_ones"], t["ident"], t["sin_table"],
                    t["cos_table"], out)


def shape_constants(c=128, h=64, w=64, heads=4, taps=12):
    eye = np.eye(c, dtype=np.float32)
    dh = c // 2
    inv_freq = 1.0 / 10000.0 ** (np.arange(0, dh, 2, dtype=np.float32) / dh)
    fh = np.arange(h, dtype=np.float32)[:, None] * inv_freq[None, :]
    fw = np.arange(w, dtype=np.float32)[:, None] * inv_freq[None, :]
    fh = np.broadcast_to(fh[:, None, :], (h, w, c // 4))
    fw = np.broadcast_to(fw[None, :, :], (h, w, c // 4))
    freqs = np.concatenate([fh, fw], axis=-1).reshape(h * w, dh).T
    scale = np.float32(1.0 / np.sqrt(np.sqrt(c // heads)))
    swap = np.zeros((c, c), np.float32)
    even = np.arange(0, c, 2)
    swap[even, even + 1] = -1.0
    swap[even + 1, even] = 1.0
    big = 2 * h + taps - 2
    up = np.zeros((h, big, taps), np.float32)
    down = np.zeros((big, h, taps), np.float32)
    for i in range(h):
        for k in range(taps):
            up[i, 2 * i + k, k] = 1.0
            down[2 * i + k, i, taps - 1 - k] = 1.0
    down = down.reshape(2, big // 2, h, taps).transpose(1, 0, 2, 3).reshape(big // 2, 2 * h, taps)
    return {
        "ident": eye,
        "centering": (eye - 1.0 / c).astype(np.float32),
        "row_select": np.tile(np.eye(32, dtype=np.float32), (3, 1)),
        "group_ones": np.kron(np.ones((c // 4, c // 4)), np.eye(4)).astype(np.float32),
        "rot_swapT": np.ascontiguousarray(swap.T),
        "sin_table": np.ascontiguousarray((np.repeat(np.sin(freqs), 2, 0) * scale).astype(np.float32)),
        "cos_table": np.ascontiguousarray((np.repeat(np.cos(freqs), 2, 0) * scale).astype(np.float32)),
        "up_places": np.concatenate([up, up]),
        "down_places": np.ascontiguousarray(down),
    }


def layout(inputs):
    g = {k: np.asarray(v) for k, v in inputs.items()}

    def split(v):
        return v.reshape(-1, 128).T

    x_projT = g["L0_conv_x_proj_w"].T
    return {
        "x": g["x"].reshape(4, 128, 4096),
        "proj_w": g["L0_conv_proj_w"],
        "in_projT": g["L0_conv_in_proj_w"].T,
        "conv_wT": g["L0_conv_conv_w"][:, 0, :].T,
        "conv_b": split(g["L0_conv_conv_b"]),
        "x_proj_cols": np.concatenate([x_projT[:, 8:]] * 3 + [x_projT[:, :8]], axis=1),
        "dt_projT": g["L0_conv_dt_proj_w"].T,
        "dt_b": split(g["L0_conv_dt_proj_b"]),
        "A_log": g["L0_conv_A_log"].reshape(2, 128, 16).transpose(1, 0, 2),
        "D": split(g["L0_conv_D"]),
        "out_projT": g["L0_conv_out_proj_w"].T,
        "next_bias": g["L1_conv_b"].reshape(128, 1),
        "up_filter": g["L1_conv_up_filter"].reshape(1, 12),
        "down_filter": g["L1_conv_down_filter"].reshape(1, 12),
        "gain": g["L1_conv_gain"].reshape(1, 1),
        "slope": g["L1_conv_slope"].reshape(1, 1),
        "clamp": g["L1_conv_clamp"].reshape(1, 1),
        "w_fc1T": g["L2_conv_w_fc1"].T,
        "ln1_w": g["L2_conv_ln1_w"].reshape(1, 32),
        "ln1_b": g["L2_conv_ln1_b"].reshape(1, 32),
        "w_fc2T": g["L2_conv_w_fc2"].T,
        "ln2_w": g["L2_conv_ln2_w"].reshape(128, 1),
        "ln2_b": g["L2_conv_ln2_b"].reshape(128, 1),
        "w_expandT": g["L2_conv_w_expand"].T,
        "w_shrinkT": g["L2_conv_w_shrink"].T,
        "grn_gamma": split(g["L2_conv_grn_gamma"]),
        "grn_beta": split(g["L2_conv_grn_beta"]),
        "gn_w": g["L3_conv_gn_w"].reshape(128, 1),
        "gn_b": g["L3_conv_gn_b"].reshape(128, 1),
        "w_qkv": g["L3_conv_w_qkv"],
        "w_qkvT": g["L3_conv_w_qkv"].T,
        "b_qkv": g["L3_conv_b_qkv"].reshape(384, 1),
        "w_projT": g["L3_conv_w_proj"].T,
        "b_proj": g["L3_conv_b_proj"].reshape(128, 1),
    }


def kernel(**inputs):
    import concourse.bacc as bacc
    from concourse.bass_utils import run_bass_kernel_spmd

    nc = bacc.Bacc("TRN2", target_bir_lowering=False, num_devices=1)
    arrays, tensors = {}, {}
    for name, a in {**layout(inputs), **shape_constants()}.items():
        a = np.ascontiguousarray(a)
        arrays[f"in_{name}"] = a
        tensors[name] = nc.dram_tensor(f"in_{name}", a.shape, mybir.dt.from_np(a.dtype), kind="ExternalInput").ap()
    out = nc.dram_tensor("out", [4, 128, 4096], mybir.dt.float32, kind="ExternalOutput").ap()
    build_program(nc, tensors, out)
    result = run_bass_kernel_spmd(nc, [arrays], core_ids=[0])
    return result.results[0]["out"].reshape(4, 128, 64, 64)
```
